# Optimizing a Trainium2 kernel written in Bass

```python
import numpy as np
import jax
import jax.numpy as jnp

def _softmax(x, axis=-1):
    return jax.nn.softmax(x, axis=axis)

def _gelu(x):
    return jax.nn.gelu(x, approximate=True)

def _silu(x):
    return jax.nn.silu(x)

def _sigmoid(x):
    return jax.nn.sigmoid(x)

def _layernorm(x, axis=-1, eps=1e-05):
    m = jnp.mean(x, axis=axis, keepdims=True)
    v = jnp.var(x, axis=axis, keepdims=True)
    return (x - m) / jnp.sqrt(v + eps)

def _scatter_add(tgt, idx, src, axis=0):
    return tgt.at[idx].add(src)

def _segment_sum(src, seg, n):
    return jax.ops.segment_sum(src, seg, n)
kernel_name = 'mk_adaln_d1_jaxref_r8_85358e'

def setup_inputs(seed: int=0):
    np.random.seed(seed)
    _w = jnp.asarray

    def _L0_attn_setup():
        import jax, jax.numpy as jnp
        import numpy as np
        B, T, D = (4, 256, 128)
        key = jax.random.key(seed)
        kx, kq, kk, kv = jax.random.split(key, 4)
        scale = 1.0 / np.sqrt(D)
        return {'x': jax.random.normal(kx, (B, T, D), dtype=jnp.float32), 'Wq': jax.random.normal(kq, (D, D), dtype=jnp.float32) * scale, 'Wk': jax.random.normal(kk, (D, D), dtype=jnp.float32) * scale, 'Wv': jax.random.normal(kv, (D, D), dtype=jnp.float32) * scale}
    _L0_attn_in = _L0_attn_setup()

    def _L0_ffn_setup():
        import jax, jax.numpy as jnp
        import numpy as np
        D = 128
        H = 256
        E = 8
        TOP_K = 2
        N_SHARED = 1
        B, S = (2, 128)
        key = jax.random.key(seed)
        ks = jax.random.split(key, 12)
        sc = 0.02
        return {'hidden': jax.random.normal(ks[0], (B, S, D), jnp.float32), 'router_w': jax.random.normal(ks[1], (D, E), jnp.float32) * sc, 'router_b': jnp.zeros((E,), jnp.float32), 'sw1': jax.random.normal(ks[2], (D, H), jnp.float32) * sc, 'sb1': jnp.zeros((H,), jnp.float32), 'sw2': jax.random.normal(ks[3], (H, D), jnp.float32) * sc, 'sb2': jnp.zeros((D,), jnp.float32), 'rw1': jax.random.normal(ks[4], (E, D, H), jnp.float32) * sc, 'rb1': jnp.zeros((E, H), jnp.float32), 'rw2': jax.random.normal(ks[5], (E, H, D), jnp.float32) * sc, 'rb2': jnp.zeros((E, D), jnp.float32)}
    _L0_ffn_in = _L0_ffn_setup()
    _L0_c = _w((lambda *s: np.random.randn(*s).astype(np.float32) * 0.05)(4, 128))
    _L0_wmod = _w((lambda *s: np.random.randn(*s).astype(np.float32) * 0.05)(128, 6 * 128) * 128 ** (-0.5))
    _d = {'L0_attn_x': _L0_attn_in['x'], 'L0_attn_Wq': _L0_attn_in['Wq'], 'L0_attn_Wk': _L0_attn_in['Wk'], 'L0_attn_Wv': _L0_attn_in['Wv'], 'L0_ffn_router_w': _L0_ffn_in['router_w'], 'L0_ffn_router_b': _L0_ffn_in['router_b'], 'L0_ffn_sw1': _L0_ffn_in['sw1'], 'L0_ffn_sb1': _L0_ffn_in['sb1'], 'L0_ffn_sw2': _L0_ffn_in['sw2'], 'L0_ffn_sb2': _L0_ffn_in['sb2'], 'L0_ffn_rw1': _L0_ffn_in['rw1'], 'L0_ffn_rb1': _L0_ffn_in['rb1'], 'L0_ffn_rw2': _L0_ffn_in['rw2'], 'L0_ffn_rb2': _L0_ffn_in['rb2'], 'L0_c': _L0_c, 'L0_wmod': _L0_wmod}
    _x0 = _d['L0_attn_x']
    _d['L0_attn_x'] = jax.random.normal(jax.random.fold_in(jax.random.key(seed), 1), (4, 512, 128), dtype=_x0.dtype)
    del _x0
    return _d

def reference(L0_attn_x, L0_attn_Wq, L0_attn_Wk, L0_attn_Wv, L0_ffn_router_w, L0_ffn_router_b, L0_ffn_sw1, L0_ffn_sb1, L0_ffn_sw2, L0_ffn_sb2, L0_ffn_rw1, L0_ffn_rb1, L0_ffn_rw2, L0_ffn_rb2, L0_c, L0_wmod):

    def _L0_attn_ref(x, Wq, Wk, Wv):
        import jax, jax.numpy as jnp
        import numpy as np
        B, T, D = (4, 256, 128)
        q = jnp.einsum('btd,od->bto', x, Wq)
        k = jnp.einsum('btd,od->bto', x, Wk)
        v = jnp.einsum('btd,od->bto', x, Wv)
        scores = jnp.einsum('bqd,bkd->bqk', q, k)
        inv_sqrt_d = 1.0 / np.sqrt(k.shape[-1]).astype(np.float32)
        weights = jax.nn.softmax(scores * inv_sqrt_d, axis=-1)
        return jnp.einsum('bqk,bkd->bqd', weights, v)

    def _L0_ffn_ref(hidden, router_w, router_b, sw1, sb1, sw2, sb2, rw1, rb1, rw2, rb2):
        import jax, jax.numpy as jnp
        import numpy as np
        D = 128
        H = 256
        E = 8
        TOP_K = 2
        N_SHARED = 1
        B, S = (2, 128)
        b, s, d = hidden.shape
        T = b * s
        flat = hidden.reshape(T, d)
        router_logits = flat @ router_w + router_b
        router_probs = jax.nn.softmax(router_logits, axis=-1)
        topk_probs, topk_idx = jax.lax.top_k(router_probs, TOP_K)
        weights = jnp.zeros_like(router_probs).at[jnp.arange(T)[:, None], topk_idx].add(topk_probs)
        sh = jax.nn.gelu(flat @ sw1 + sb1, approximate=False)
        shared_out = (sh @ sw2 + sb2) / N_SHARED
        h1 = jax.nn.gelu(jnp.einsum('td,edh->teh', flat, rw1) + rb1[None], approximate=False)
        expert_out = jnp.einsum('teh,ehd->ted', h1, rw2) + rb2[None]
        mixed = jnp.einsum('ted,te->td', expert_out, weights)
        return (shared_out + mixed).reshape(b, s, d)
    x = L0_attn_x
    mod = (_silu(L0_c) @ L0_wmod).reshape(L0_c.shape[0], 6, 1, -1)
    sa, ca, ga, sb, cb, gb = (mod[:, 0], mod[:, 1], mod[:, 2], mod[:, 3], mod[:, 4], mod[:, 5])
    ga = (2 * (ga >= 0) - 1) * jnp.maximum(jnp.abs(ga), 0.25)
    gb = (2 * (gb >= 0) - 1) * jnp.maximum(jnp.abs(gb), 0.25)
    h = _layernorm(x, axis=-1) * (1 + ca) + sa
    x = x + ga * _L0_attn_ref(h, L0_attn_Wq, L0_attn_Wk, L0_attn_Wv)
    h = _layernorm(x, axis=-1) * (1 + cb) + sb
    x = x + gb * _L0_ffn_ref(h, L0_ffn_router_w, L0_ffn_router_b, L0_ffn_sw1, L0_ffn_sb1, L0_ffn_sw2, L0_ffn_sb2, L0_ffn_rw1, L0_ffn_rb1, L0_ffn_rw2, L0_ffn_rb2)
    return x

_drawn_inputs = setup_inputs


def setup_inputs(seed=0):
    import zlib

    import numpy as np

    out = dict(_drawn_inputs(seed))
    spreads = {'L0_ffn_router_b': (0.0, 0.8),
     'L0_ffn_sb1': (0.0, 0.8),
     'L0_ffn_sb2': (0.0, 0.287),
     'L0_ffn_rb1': (0.0, 0.8),
     'L0_ffn_rb2': (0.0, 0.8)}
    factors = {'L0_ffn_router_w': 8.0,
     'L0_ffn_sw1': 6.067,
     'L0_ffn_sw2': 5.556,
     'L0_ffn_rw1': 8.0,
     'L0_ffn_rw2': 8.0}
    for name, (base, spread) in spreads.items():
        noise = np.random.default_rng([zlib.crc32(name.encode()), seed]).standard_normal(out[name].shape)
        drawn = base * np.exp(spread * noise) if base else spread * noise
        out[name] = jnp.asarray(drawn.astype(out[name].dtype))
    for name, factor in factors.items():
        out[name] = (out[name] * factor).astype(out[name].dtype)
    return out
```

```python
import concourse.bass as bass
from concourse import mybir
from contextlib import ExitStack

F32 = mybir.dt.float32
F32R = mybir.dt.float32r
ALU = mybir.AluOpType
ACT = mybir.ActivationFunctionType
AX = mybir.AxisListType

P = 128
EPS = 1e-5


def adaln_attention_moe(nc, x, early, late, router_b, w1, w2, rb2, out):
    B, S, D = x.shape
    T = S // P
    E = rb2.shape[0]
    NE = E + 1
    HC = w1.shape[2] // P
    NK = NE * HC
    assert D == P and S == 512 and w1.shape[1] == NE
    SCALE = float(D) ** -0.5
    KW = 64 + E
    TOKENS = B * T

    with ExitStack() as ctx:
        def sb(name, shape, dt=F32):
            return ctx.enter_context(nc.sbuf_tensor(name, shape, dt))

        def sem(name):
            return ctx.enter_context(nc.semaphore(name))

        def full(t):
            return t.bitcast(F32)

        early_sb = sb("early_sb", [P, early.shape[1]])
        late_sb = sb("late_sb", [P, late.shape[1]])
        c_t = early_sb[:, 0:B]
        wmod = early_sb[:, B:B + 6 * D].rearrange("p (m n) -> p m n", m=6)
        o = 0
        wq = late_sb[:, o:o + D]; o += D
        wk = late_sb[:, o:o + D]; o += D
        wv_t = late_sb[:, o:o + D]; o += D
        router_w = late_sb[:, o:o + E]; o += E
        b1 = late_sb[:, o:o + NK].rearrange("p (e c) -> p e c", c=HC); o += NK
        sb2 = late_sb[:, o:o + 1]
        rb_sb = sb("rb_sb", [P, E])
        rb2_sb = sb("rb2_sb", [KW, D])
        rb2_hi = sb("rb2_hi", [KW, D], F32R)
        rb2_st = sb("rb2_st", [KW, D], F32R)
        ident = sb("ident", [P, P])
        before = sb("before", [P, E, E])
        picks = sb("picks", [KW, E])
        pick = sb("pick", [KW, E, P], F32R)
        half = sb("half", [P, T])
        w1_sb = sb("w1_sb", [P, NE, HC * P])
        w1_hi = sb("w1_hi", [P, NE, HC * P], F32R)
        w1_lo = sb("w1_lo", [P, NE, HC * P], F32R)
        w2_sb = sb("w2_sb", [P, NE, HC * D])
        w2_hi = sb("w2_hi", [P, NE, HC * D], F32R)
        w2_lo = sb("w2_lo", [P, NE, HC * D], F32R)
        silu_e = sb("silu_e", [P, B])
        silu_d = sb("silu_d", [P, B])
        silu_r = sb("silu_r", [P, B])
        silu_c = sb("silu_c", [P, B, P])
        rows = sb("rows", [P, B, 3, D])
        ca1 = sb("ca1", [P, B, D])
        ga_s = sb("ga_s", [P, B, D])
        ga_m = sb("ga_m", [P, B, D])
        ga_f = rows[:, :, 2]
        cols = sb("cols", [P, 3, B])
        cb1 = sb("cb1", [P, B])
        gb_s = sb("gb_s", [P, B])
        gb_m = sb("gb_m", [P, B])
        gb_f = sb("gb_f", [P, B])
        g_hi = sb("g_hi", [P, D], F32R)
        g_lo = sb("g_lo", [P, D], F32R)
        g_f = sb("g_f", [P, D])
        wvg = ga_s
        wvg_hi = sb("wvg_hi", [P, B, D], F32R)
        wvg_lo = sb("wvg_lo", [P, B, D], F32R)
        x_sb = sb("x_sb", [P, B, T, D])
        x1_sb = sb("x1_sb", [P, B, T, D])
        stats = sb("stats", [P, 2, B, T, 6])
        mv = sb("mv", [P, 2, B, T, 2])
        ve = sb("ve", [P, 2, B, T])
        rstd = sb("rstd", [P, 2, B, T])
        n_sb = sb("n_sb", [P, 2, T, D])
        nh_sb = sb("nh_sb", [P, 2, 2, T, D])
        nc_sb, h_sb = nh_sb[:, 0], nh_sb[:, 1]
        h_hi = sb("h_hi", [P, 2, T, D], F32R)
        h_lo = sb("h_lo", [P, 2, T, D], F32R)
        ht_hi = sb("ht_hi", [P, 2, S], F32R)
        ht_lo = sb("ht_lo", [P, 2, S], F32R)
        q_hi = sb("q_hi", [P, 2, S], F32R)
        q_lo = sb("q_lo", [P, 2, S], F32R)
        nmax = sb("nmax", [P, B, T])
        rsum = sb("rsum", [P, B, T])
        rinv = sb("rinv", [P, B, T])
        p_sb = sb("p_sb", [P, T, S])
        pt_hi = sb("pt_hi", [P, T, S], F32R)
        pt_lo = sb("pt_lo", [P, T, S], F32R)
        ct_hi = sb("ct_hi", [P, S], F32R)
        ct_lo = sb("ct_lo", [P, S], F32R)
        n2_sb = sb("n2_sb", [P, T, D])
        lg = sb("lg", [P, B, T, E])
        lmax = sb("lmax", [P, B, T])
        le = sb("le", [P, B, T, E])
        ex = sb("ex", [P, B, T, E])
        es = sb("es", [P, B, T])
        er = sb("er", [P, B, T])
        pr = sb("pr", [P, B, T, E])
        gt = sb("gt", [P, T, E, E])
        ge = sb("ge", [P, T, E, E])
        gb = sb("gb", [P, T, E, E])
        gm = sb("gm", [P, T, E, E])
        rank = sb("rank", [P, T, E])
        wt = sb("wt", [P, T, E])
        wst = sb("wst", [P, T, KW], F32R)
        wt_t = sb("wt_t", [KW, B, S], F32R)
        h2 = sb("h2", [P, 2, S])
        h2_hi = sb("h2_hi", [P, B, S], F32R)
        h2_lo = sb("h2_lo", [P, B, S], F32R)
        SL = 4
        act_sb = p_sb
        t_sb = nh_sb[:].rearrange("p a b t d -> p (a b) (t d)")
        t_hi, t_lo = pt_hi, pt_lo
        out_sb = x_sb[:, 0:2]
        y_sb = x_sb[:, 2:4].rearrange("p b t d -> p b (t d)")

        bank = [ctx.enter_context(nc.psum_tensor(f"bank{i}", [P, 512], F32)) for i in range(8)]
        s_ps = bank[0:2]
        t_ps = bank[2:4]
        a_ps, q_ps, c_ps, o_ps = bank[4:8]
        hid_ps = bank[0:3]
        wb_ps = bank[3:5]
        y_ps = bank[5]
        acc_ps = bank[6:8]

        early_in = sem("early_in"); x_in = [sem(f"x_in{b}") for b in range(B)]
        late_in = sem("late_in"); small_in = sem("small_in")
        w1_in = sem("w1_in"); w2_in = sem("w2_in"); stored = [sem(f"stored{i}") for i in range(2)]
        consts = sem("consts"); silu_exp = sem("silu_exp"); silu = sem("silu")
        rows_mm = sem("rows_mm"); rows_ev = sem("rows_ev"); cols_mm = sem("cols_mm"); cols_ev = sem("cols_ev")
        modded = sem("modded"); colmod = sem("colmod")
        g_mm = sem("g_mm"); g_split = sem("g_split"); wv_split = sem("wv_split")
        w_hi = sem("w_hi"); w_lo = sem("w_lo"); rb2_sem = sem("rb2_sem"); picked = sem("picked")
        st1 = sem("st1"); mv1 = sem("mv1"); rs1 = sem("rs1"); n1 = sem("n1"); hmul = sem("hmul"); hadd = sem("hadd")
        hhi = sem("hhi"); hlo = sem("hlo"); ht_mm = sem("ht_mm"); hthi = sem("hthi"); htlo = sem("htlo")
        q_mm = sem("q_mm"); qhi = sem("qhi"); qlo = sem("qlo")
        s_mm = sem("s_mm"); nmx = sem("nmx"); probs = sem("probs"); pt_mm = sem("pt_mm"); pthi = sem("pthi"); ptlo = sem("ptlo")
        c_mm = sem("c_mm"); chi = sem("chi"); clo = sem("clo"); o_mm = sem("o_mm"); rinvd = sem("rinvd"); x1d = sem("x1d")
        st2 = sem("st2"); mv2 = sem("mv2"); rs2 = sem("rs2"); n2 = sem("n2"); n2t_mm = sem("n2t_mm")
        h2d = sem("h2d"); h2hi = sem("h2hi"); h2lo = sem("h2lo")
        l_mm = sem("l_mm"); rt = sem("rt"); rexp = sem("rexp"); lmx = sem("lmx"); wsd = sem("wsd"); wt_mm = sem("wt_mm"); wtd = sem("wtd")
        hid_mm = sem("hid_mm"); gelu = sem("gelu"); wb_mm = sem("wb_mm"); wtd_k = sem("wtd_k"); thi = sem("thi"); tlo = sem("tlo")
        acc_k = sem("acc_k"); yev = sem("yev"); y_mm = sem("y_mm"); outd = sem("outd")

        block = ctx.enter_context(nc.Block())

        def weighed(K):
            b, k = divmod(K, NK)
            return b * (NK - HC) + max(0, k + 1 - HC)

        @block.sync
        def _(sp):
            sp.dma_start(early_sb[:], early).then_inc(early_in, 16)
            for b in range(B):
                sp.dma_start(x_sb[:, b], x[b].rearrange("(p t) d -> p t d", t=T)).then_inc(x_in[b], 16)
                if b == 0:
                    sp.dma_start(late_sb[:], late).then_inc(late_in, 16)
            sp.dma_start(w1_sb[:], w1).then_inc(w1_in, 16)
            sp.dma_start(w2_sb[:], w2).then_inc(w2_in, 16)
            for b in range(B):
                sp.wait_ge(outd, b + 1)
                sp.dma_start(out[b].rearrange("(p t) d -> p t d", t=T), out_sb[:, b % 2]).then_inc(stored[b % 2], 16)
            for i in range(2):
                sp.wait_ge(stored[i], 16 * ((B + 1 - i) // 2))

        @block.gpsimd
        def _(pool):
            pool.memset(ident[:], 0.0).then_inc(consts, 1)
            pool.memset(picks[:], 0.0).then_inc(consts, 1)
            pool.memset(before[:], 1.0).then_inc(consts, 1)
            pool.memset(half[:], -0.5).then_inc(consts, 1)
            pool.memset(full(wst[:]), 0.0).then_inc(consts, 1)
            pool.memset(rb2_sb[:], 0.0).then_inc(consts, 1)
            pool.wait_ge(consts, 6)
            pool.affine_select(out=ident[:], in_=ident[:], compare_op=ALU.not_equal, fill=1.0, base=0,
                               pattern=[[-1, P]], channel_multiplier=1).then_inc(consts, 1)
            pool.affine_select(out=before[:], in_=before[:], compare_op=ALU.is_ge, fill=0.0, base=-1,
                               pattern=[[1, E], [-1, E]], channel_multiplier=0).then_inc(consts, 1)
            for n, shift in enumerate((0, 32)):
                if n:
                    pool.wait_ge(consts, 9)
                pool.affine_select(out=picks[:], in_=picks[:], compare_op=ALU.not_equal, fill=1.0, base=-shift,
                                   pattern=[[-1, E]], channel_multiplier=1).then_inc(consts, 1)
            for n, q in enumerate((0, 32, 64)):
                pool.dma_start(rb2_sb[q:q + E, :], rb2).then_inc(small_in, 16)
            pool.dma_start(rb_sb[:], router_b.to_broadcast([P, E])).then_inc(small_in, 16)

            def rsqrt_var(n, b, mvs, rss):
                pool.wait_ge(mvs, b + 1)
                pool.tensor_scalar(ve[:, n, b], mv[:, n, b, :, 1], EPS, 0.0, ALU.add, ALU.add).then_inc(rss, 1)
                pool.wait_ge(rss, 2 * b + 1)
                pool.tensor_tensor(rstd[:, n, b], ve[:, n, b], half[:], ALU.pow).then_inc(rss, 1)

            def modulate(b):
                pool.wait_ge(n1, b + 1)
                if b == 0:
                    pool.wait_ge(modded, 1)
                rep = lambda a: a[:, b:b + 1].to_broadcast([P, T, D])
                pool.tensor_tensor(nc_sb[:, b % 2], n_sb[:, b % 2], rep(ca1), ALU.mult).then_inc(hmul, 1)
                pool.wait_ge(hmul, b + 1)
                if b >= 2:
                    pool.wait_ge(ht_mm, b - 1)
                    pool.wait_ge(hhi, b - 1)
                    pool.wait_ge(hlo, b - 1)
                pool.tensor_tensor(h_sb[:, b % 2], nc_sb[:, b % 2], rows[:, b:b + 1, 0].to_broadcast([P, T, D]), ALU.add).then_inc(hadd, 1)

            def split_h(b):
                pool.wait_ge(hhi, b + 1)
                pool.wait_ge(hadd, b + 1)
                if b >= 2:
                    pool.wait_ge(c_mm, b - 1)
                pool.tensor_tensor(h_lo[:, b % 2], h_sb[:, b % 2], full(h_hi[:, b % 2]), ALU.subtract).then_inc(hlo, 1)

            def weights_lo(e):
                pool.wait_ge(w_hi, e + 1)
                pool.tensor_tensor(w1_lo[:, e], w1_sb[:, e], full(w1_hi[:, e]), ALU.subtract)
                pool.tensor_tensor(w2_lo[:, e], w2_sb[:, e], full(w2_hi[:, e]), ALU.subtract).then_inc(w_lo, 1)

            rsqrt_var(0, 0, mv1, rs1)
            modulate(0)
            rsqrt_var(0, 1, mv1, rs1)
            split_h(0)
            modulate(1)
            for b in range(B):
                if b + 2 < B:
                    rsqrt_var(0, b + 2, mv1, rs1)
                if b + 1 < B:
                    split_h(b + 1)
                if b + 2 < B:
                    modulate(b + 2)
                if b == 1:
                    for e in range(0, 3):
                        weights_lo(e)
                rsqrt_var(1, b, mv2, rs2)
            for e in range(3, NE):
                weights_lo(e)

        @block.scalar
        def _(act):
            act.wait_ge(early_in, 16)
            act.activation(silu_e[:], c_t, ACT.Exp, scale=-1.0).then_inc(silu_exp, 1)
            for b in range(B):
                act.wait_ge(rows_mm, b + 1)
                act.activation(rows[:, b].rearrange("p m d -> p (m d)"), bank[b][:, 0:3 * D], ACT.Copy).then_inc(rows_ev, 1)

            def h_split_hi(b):
                act.wait_ge(hadd, b + 1)
                if b >= 2:
                    act.wait_ge(c_mm, b - 1)
                    act.wait_ge(hlo, b - 1)
                act.activation(h_hi[:, b % 2], h_sb[:, b % 2], ACT.Copy).then_inc(hhi, 1)

            def ht_split_hi(b):
                act.wait_ge(ht_mm, b + 1)
                if b >= 2:
                    act.wait_ge(s_mm, T * (b - 1))
                    act.wait_ge(htlo, b - 1)
                act.activation(ht_hi[:, b % 2], a_ps[:], ACT.Copy).then_inc(hthi, 1)

            def q_split_hi(b):
                act.wait_ge(q_mm, b + 1)
                if b >= 2:
                    act.wait_ge(s_mm, T * (b - 1))
                    act.wait_ge(qlo, b - 1)
                act.activation(q_hi[:, b % 2], q_ps[:], ACT.Copy).then_inc(qhi, 1)

            def exps(b, t):
                n = T * b + t
                act.wait_ge(nmx, n + 1)
                if b:
                    act.wait_ge(pt_mm, n - T + 1)
                act.activation(p_sb[:, t], s_ps[n % 2][:], ACT.Exp, bias=nmax[:, b, t:t + 1],
                               accum_out=rsum[:, b, t:t + 1]).then_inc(probs, 1)

            def pt_split_hi(b, t):
                n = T * b + t
                act.wait_ge(pt_mm, n + 1)
                if b:
                    act.wait_ge(c_mm, b)
                    act.wait_ge(ptlo, T * b)
                act.activation(pt_hi[:, :, t * P:(t + 1) * P], t_ps[n % 2][:].rearrange("p (k q) -> p k q", k=T),
                               ACT.Copy).then_inc(pthi, 1)

            def c_split_hi(b):
                act.wait_ge(c_mm, b + 1)
                if b:
                    act.wait_ge(o_mm, b)
                    act.wait_ge(clo, b)
                act.activation(ct_hi[:], c_ps[:], ACT.Copy).then_inc(chi, 1)

            def h2_make(b):
                act.wait_ge(n2t_mm, b + 1)
                if b == 0:
                    act.wait_ge(colmod, 1)
                if b >= 2:
                    act.wait_ge(h2lo, b - 1)
                    act.wait_ge(l_mm, b - 1)
                act.activation(h2[:, b % 2], a_ps[:], ACT.Identity, scale=cb1[:, b:b + 1], bias=cols[:, 0, b:b + 1]).then_inc(h2d, 1)
                act.wait_ge(h2d, b + 1)
                act.activation(h2_hi[:, b], h2[:, b % 2], ACT.Copy).then_inc(h2hi, 1)

            def router_exp(b):
                act.wait_ge(lmx, b + 1)
                act.activation(ex[:, b], le[:, b], ACT.Exp).then_inc(rexp, 1)

            h_split_hi(0)
            ht_split_hi(0)
            q_split_hi(0)
            for b in range(B):
                exps(b, 0)
                if b + 1 < B:
                    h_split_hi(b + 1)
                exps(b, 1)
                exps(b, 2)
                pt_split_hi(b, 0)
                exps(b, 3)
                pt_split_hi(b, 1)
                if b + 1 < B:
                    ht_split_hi(b + 1)
                pt_split_hi(b, 2)
                if b + 1 < B:
                    q_split_hi(b + 1)
                pt_split_hi(b, 3)
                if b:
                    h2_make(b - 1)
                    router_exp(b - 1)
                c_split_hi(b)
            h2_make(B - 1)
            router_exp(B - 1)

            def gelus(K):
                b, k = divmod(K, NK)
                act.wait_ge(hid_mm, K + 1)
                if K >= SL:
                    if (K - SL) % NK < HC:
                        act.wait_ge(thi, K - SL + 1)
                        act.wait_ge(tlo, K - SL + 1)
                    else:
                        act.wait_ge(wtd_k, weighed(K - SL))
                act.activation(act_sb[:, K % SL], hid_ps[K % 3][:], ACT.Gelu, bias=b1[:, k // HC, k % HC:k % HC + 1]).then_inc(gelu, 1)

            def split_hi(K):
                k = K % NK
                if k < HC:
                    act.wait_ge(gelu, K + 1)
                else:
                    act.wait_ge(wtd_k, weighed(K))
                if K >= SL:
                    act.wait_ge(acc_k, K - SL + 1)
                    act.wait_ge(tlo, K - SL + 1)
                src = act_sb if k < HC else t_sb
                act.activation(t_hi[:, K % SL], src[:, K % SL], ACT.Copy).then_inc(thi, 1)

            gelus(0)
            for K in range(B * NK):
                if K + 1 < B * NK:
                    gelus(K + 1)
                split_hi(K)

        @block.vector
        def _(dve):
            dve.wait_ge(silu_exp, 1)
            dve.tensor_scalar(silu_d[:], silu_e[:], 1.0, None, ALU.add).then_inc(silu, 1)
            dve.wait_ge(silu, 1)
            dve.reciprocal(silu_r[:], silu_d[:]).then_inc(silu, 1)
            dve.wait_ge(silu, 2)
            dve.tensor_tensor(silu_c[:], silu_r[:, :, None].to_broadcast([P, B, P]), c_t[:, :, None].to_broadcast([P, B, P]),
                              ALU.mult).then_inc(silu, 1)

            def layer_stats(n, b, src, sts, mvs):
                for t in range(T):
                    i = dve.bn_stats(stats[:, n, b, t], src[:, b, t])
                i.then_inc(sts, 1)
                dve.wait_ge(sts, b + 1)
                for t in range(T):
                    i = dve.bn_aggr(mv[:, n, b, t], stats[:, n, b, t])
                i.then_inc(mvs, 1)

            def norm1(b):
                dve.wait_ge(rs1, 2 * b + 2)
                if b >= 2:
                    dve.wait_ge(hmul, b - 1)
                for t in range(T):
                    i = dve.tensor_scalar(n_sb[:, b % 2, t], x_sb[:, b, t], mv[:, 0, b, t, 0:1], rstd[:, 0, b, t:t + 1],
                                          ALU.subtract, ALU.mult)
                i.then_inc(n1, 1)

            def ht_split_lo(b):
                dve.wait_ge(hthi, b + 1)
                if b >= 2:
                    dve.wait_ge(s_mm, T * (b - 1))
                dve.tensor_tensor(ht_lo[:, b % 2], a_ps[:], full(ht_hi[:, b % 2]), ALU.subtract).then_inc(htlo, 1)

            def q_split_lo(b):
                dve.wait_ge(qhi, b + 1)
                if b >= 2:
                    dve.wait_ge(s_mm, T * (b - 1))
                dve.tensor_tensor(q_lo[:, b % 2], q_ps[:], full(q_hi[:, b % 2]), ALU.subtract).then_inc(qlo, 1)

            def row_max(b, t):
                n = T * b + t
                dve.wait_ge(s_mm, n + 1)
                dve.tensor_reduce(nmax[:, b, t:t + 1], s_ps[n % 2][:], AX.X, ALU.max, negate=True).then_inc(nmx, 1)

            def pt_split_lo(b, t):
                n = T * b + t
                dve.wait_ge(pthi, n + 1)
                if b:
                    dve.wait_ge(c_mm, b)
                dve.tensor_tensor(pt_lo[:, :, t * P:(t + 1) * P], t_ps[n % 2][:].rearrange("p (k q) -> p k q", k=T),
                                  full(pt_hi[:, :, t * P:(t + 1) * P]), ALU.subtract).then_inc(ptlo, 1)

            def c_split_lo(b):
                dve.wait_ge(chi, b + 1)
                if b:
                    dve.wait_ge(o_mm, b)
                dve.tensor_tensor(ct_lo[:], c_ps[:], full(ct_hi[:]), ALU.subtract).then_inc(clo, 1)

            def residual(b):
                dve.wait_ge(probs, T * (b + 1))
                dve.reciprocal(rinv[:, b], rsum[:, b]).then_inc(rinvd, 1)
                dve.wait_ge(rinvd, b + 1)
                dve.wait_ge(o_mm, b + 1)
                for t in range(T):
                    i = dve.scalar_tensor_tensor(x1_sb[:, b, t], o_ps[:, t * D:(t + 1) * D], rinv[:, b, t:t + 1],
                                                 x_sb[:, b, t], ALU.mult, ALU.add)
                i.then_inc(x1d, 1)
                dve.wait_ge(x1d, b + 1)
                layer_stats(1, b, x1_sb, st2, mv2)

            def norm2(b):
                dve.wait_ge(rs2, 2 * b + 2)
                if b:
                    dve.wait_ge(n2t_mm, b)
                for t in range(T):
                    i = dve.tensor_scalar(n2_sb[:, t], x1_sb[:, b, t], mv[:, 1, b, t, 0:1], rstd[:, 1, b, t:t + 1],
                                          ALU.subtract, ALU.mult)
                i.then_inc(n2, 1)

            def h2_split_lo(b):
                dve.wait_ge(h2hi, b + 1)
                dve.tensor_tensor(h2_lo[:, b], h2[:, b % 2], full(h2_hi[:, b]), ALU.subtract).then_inc(h2lo, 1)

            rtn = [0]

            def step(i):
                i.then_inc(rt, 1)
                rtn[0] += 1
                dve.wait_ge(rt, rtn[0])

            def router_logits(b):
                dve.wait_ge(l_mm, b + 1)
                if b == 0:
                    dve.wait_ge(small_in, 64)
                step(dve.tensor_tensor(lg[:, b], o_ps[:, 0:T * E].rearrange("p (t e) -> p t e", t=T),
                                       rb_sb[:, None, :].to_broadcast([P, T, E]), ALU.add))
                step(dve.tensor_reduce(lmax[:, b], lg[:, b], AX.X, ALU.max))
                dve.tensor_tensor(le[:, b], lg[:, b], lmax[:, b, :, None].to_broadcast([P, T, E]), ALU.subtract).then_inc(lmx, 1)

            def router_weights(b):
                dve.wait_ge(rexp, b + 1)
                step(dve.tensor_reduce(es[:, b], ex[:, b], AX.X, ALU.add))
                step(dve.reciprocal(er[:, b], es[:, b]))
                step(dve.tensor_tensor(pr[:, b], ex[:, b], er[:, b, :, None].to_broadcast([P, T, E]), ALU.mult))
                pj = pr[:, b, :, None, :].to_broadcast([P, T, E, E])
                pe_ = pr[:, b, :, :, None].to_broadcast([P, T, E, E])
                dve.tensor_tensor(gt[:], pj, pe_, ALU.is_gt)
                step(dve.tensor_tensor(ge[:], pj, pe_, ALU.is_ge))
                step(dve.tensor_tensor(gb[:], ge[:], before[:, None].to_broadcast([P, T, E, E]), ALU.mult))
                step(dve.tensor_tensor(gm[:], gb[:], gt[:], ALU.max))
                step(dve.tensor_reduce(rank[:], gm[:], AX.X, ALU.add))
                step(dve.scalar_tensor_tensor(wt[:], rank[:], 1.5, pr[:, b], ALU.is_lt, ALU.mult))
                if b:
                    dve.wait_ge(wt_mm, b)
                step(dve.tensor_copy(wst[:, :, 0:E], wt[:]))
                dve.tensor_copy(wst[:, :, 64:64 + E], wt[:])
                dve.tensor_tensor(wst[:, :, 32:32 + E], wt[:], full(wst[:, :, 0:E]), ALU.subtract).then_inc(wsd, 1)

            def weights_t(b):
                dve.wait_ge(wt_mm, b + 1)
                dve.tensor_copy(wt_t[:, b], q_ps[0:KW, :]).then_inc(wtd, 1)

            def weights_hi(e):
                if e == 0:
                    dve.wait_ge(w1_in, 16)
                    dve.wait_ge(w2_in, 16)
                dve.tensor_copy(w1_hi[:, e], w1_sb[:, e])
                dve.tensor_copy(w2_hi[:, e], w2_sb[:, e]).then_inc(w_hi, 1)

            dve.wait_ge(x_in[0], 16)
            layer_stats(0, 0, x_sb, st1, mv1)
            dve.wait_ge(g_mm, 1)
            dve.tensor_scalar(g_f[:], q_ps[:, 0:D], SCALE, None, ALU.mult).then_inc(g_split, 1)
            dve.wait_ge(g_split, 1)
            dve.tensor_copy(g_hi[:], g_f[:]).then_inc(g_split, 1)
            dve.wait_ge(g_split, 2)
            dve.tensor_tensor(g_lo[:], g_f[:], full(g_hi[:]), ALU.subtract).then_inc(g_split, 1)
            norm1(0)
            dve.wait_ge(rows_ev, B)
            dve.tensor_scalar(ca1[:], rows[:, :, 1], 1.0, None, ALU.add).then_inc(modded, 1)
            dve.wait_ge(x_in[1], 16)
            layer_stats(0, 1, x_sb, st1, mv1)
            dve.tensor_scalar(ga_s[:], rows[:, :, 2], 0.0, 2.0, ALU.is_ge, ALU.mult).then_inc(wv_split, 1)
            dve.wait_ge(wv_split, 1)
            dve.tensor_scalar(ga_m[:], ga_s[:], -1.0, None, ALU.add).then_inc(wv_split, 1)
            dve.wait_ge(wv_split, 2)
            dve.tensor_tensor(ga_s[:], ga_m[:], rows[:, :, 2], ALU.mult).then_inc(wv_split, 1)
            dve.wait_ge(wv_split, 3)
            dve.scalar_tensor_tensor(ga_f, ga_s[:], 0.25, ga_m[:], ALU.max, ALU.mult).then_inc(wv_split, 1)
            ht_split_lo(0)
            norm1(1)
            dve.wait_ge(wv_split, 4)
            dve.tensor_tensor(wvg[:], ga_f, wv_t[:, None, :].to_broadcast([P, B, D]), ALU.mult).then_inc(wv_split, 1)
            q_split_lo(0)
            dve.wait_ge(wv_split, 5)
            dve.tensor_copy(wvg_hi[:], wvg[:]).then_inc(wv_split, 1)
            dve.wait_ge(wv_split, 6)
            dve.tensor_tensor(wvg_lo[:], wvg[:], full(wvg_hi[:]), ALU.subtract).then_inc(wv_split, 1)
            dve.wait_ge(cols_mm, 1)
            dve.tensor_copy(cols[:], a_ps[:, 0:3 * B].rearrange("p (m b) -> p m b", m=3)).then_inc(cols_ev, 1)
            for b in range(B):
                row_max(b, 0)
                row_max(b, 1)
                if b == 0:
                    dve.wait_ge(cols_ev, 1)
                    dve.tensor_scalar(cb1[:], cols[:, 1], 1.0, None, ALU.add)
                    dve.tensor_scalar(gb_s[:], cols[:, 2], 0.0, 2.0, ALU.is_ge, ALU.mult).then_inc(cols_ev, 1)
                    dve.wait_ge(cols_ev, 2)
                    dve.tensor_scalar(gb_m[:], gb_s[:], -1.0, None, ALU.add).then_inc(cols_ev, 1)
                    dve.wait_ge(cols_ev, 3)
                    dve.tensor_tensor(gb_s[:], gb_m[:], cols[:, 2], ALU.mult).then_inc(cols_ev, 1)
                    dve.wait_ge(cols_ev, 4)
                    dve.scalar_tensor_tensor(gb_f[:], gb_s[:], 0.25, gb_m[:], ALU.max, ALU.mult).then_inc(colmod, 1)
                    dve.wait_ge(small_in, 64)
                    dve.tensor_copy(rb2_hi[:], rb2_sb[:]).then_inc(rb2_sem, 1)
                    dve.wait_ge(rb2_sem, 1)
                    dve.tensor_copy(rb2_st[0:64], full(rb2_hi[0:64]))
                    dve.tensor_tensor(rb2_st[64:KW], rb2_sb[64:KW], full(rb2_hi[64:KW]), ALU.subtract).then_inc(rb2_sem, 1)
                    dve.wait_ge(consts, 10)
                    dve.tensor_copy(pick[:], picks[:, :, None].to_broadcast([KW, E, P])).then_inc(picked, 1)
                else:
                    residual(b - 1)
                row_max(b, 2)
                if b + 2 < B:
                    dve.wait_ge(x_in[b + 2], 16)
                    layer_stats(0, b + 2, x_sb, st1, mv1)
                pt_split_lo(b, 0)
                row_max(b, 3)
                if b:
                    norm2(b - 1)
                pt_split_lo(b, 1)
                if b + 1 < B:
                    ht_split_lo(b + 1)
                pt_split_lo(b, 2)
                if b + 1 < B:
                    q_split_lo(b + 1)
                if b + 2 < B:
                    norm1(b + 2)
                pt_split_lo(b, 3)
                if b:
                    router_logits(b - 1)
                    h2_split_lo(b - 1)
                    router_weights(b - 1)
                c_split_lo(b)
                if b:
                    weights_t(b - 1)
                for e in range(NE * b // B, NE * (b + 1) // B):
                    weights_hi(e)
            residual(B - 1)
            norm2(B - 1)
            router_logits(B - 1)

            def weigh(K):
                b, k = divmod(K, NK)
                if k < HC:
                    return
                e = k // HC
                dve.wait_ge(gelu, K + 1)
                dve.wait_ge(wb_mm, b * E + e)
                if K >= SL:
                    dve.wait_ge(thi, K - SL + 1)
                dve.tensor_tensor(t_sb[:, K % SL], act_sb[:, K % SL], wb_ps[(b * E + e) % 2][:], ALU.mult).then_inc(wtd_k, 1)

            def split_lo(K):
                k = K % NK
                dve.wait_ge(thi, K + 1)
                if K >= SL:
                    dve.wait_ge(acc_k, K - SL + 1)
                src = act_sb if k < HC else t_sb
                dve.tensor_tensor(t_lo[:, K % SL], src[:, K % SL], full(t_hi[:, K % SL]), ALU.subtract).then_inc(tlo, 1)

            def y_evac(b):
                dve.wait_ge(acc_k, (b + 1) * NK)
                if b >= 2:
                    dve.wait_ge(y_mm, b - 1)
                dve.tensor_scalar(y_sb[:, b % 2], acc_ps[b % 2][:], sb2, gb_f[:, b:b + 1], ALU.add, ALU.mult).then_inc(yev, 1)

            def output(b):
                dve.wait_ge(y_mm, b + 1)
                if b >= 2:
                    dve.wait_ge(stored[b % 2], 16 * (b // 2))
                dve.tensor_tensor(out_sb[:, b % 2].rearrange("p t d -> p (t d)"), y_ps[:],
                                  x1_sb[:, b].rearrange("p t d -> p (t d)"), ALU.add).then_inc(outd, 1)

            for K in range(B * NK):
                b, k = divmod(K, NK)
                if K + 1 < B * NK:
                    weigh(K + 1)
                split_lo(K)
                if K == 3:
                    h2_split_lo(B - 1)
                    router_weights(B - 1)
                if K == 8:
                    weights_t(B - 1)
                if b and k == 4:
                    y_evac(b - 1)
                if b and k == 6:
                    output(b - 1)
            y_evac(B - 1)
            output(B - 1)

        @block.tensor
        def _(pe):
            def product(ps, lhs, rhs, start=True, stop=True):
                pe.matmul(ps, lhs[0], rhs[0], start=start, stop=False)
                pe.matmul(ps, lhs[0], rhs[1], start=False, stop=False)
                return pe.matmul(ps, lhs[1], rhs[0], start=False, stop=stop)

            pe.wait_ge(silu, 3)
            for b in range(B):
                pe.matmul(bank[b][:, 0:3 * D], silu_c[:, b], wmod[:, 0:3].rearrange("p m n -> p (m n)"),
                          start=True, stop=True).then_inc(rows_mm, 1)
            pe.wait_ge(late_in, 16)
            pe.matmul(q_ps[:, 0:D], wq, wk, start=True, stop=True).then_inc(g_mm, 1)

            def h_transposes(b):
                pe.wait_ge(hadd, b + 1)
                if b == 0:
                    pe.wait_ge(consts, 7)
                else:
                    pe.wait_ge(htlo, b)
                    if b >= 3:
                        pe.wait_ge(h2d, b - 2)
                    elif b == 1:
                        pe.wait_ge(cols_ev, 1)
                for t in range(T):
                    i = pe.transpose(a_ps[:, t * P:(t + 1) * P], h_sb[:, b % 2, t], ident[:])
                i.then_inc(ht_mm, 1)

            def q_project(b):
                pe.wait_ge(hthi, b + 1)
                pe.wait_ge(htlo, b + 1)
                if b == 0:
                    pe.wait_ge(g_split, 3)
                else:
                    pe.wait_ge(qlo, b)
                    if b >= 3:
                        pe.wait_ge(wtd, b - 2)
                product(q_ps[:], (g_hi[:], g_lo[:]), (ht_hi[:, b % 2], ht_lo[:, b % 2])).then_inc(q_mm, 1)

            def scores(b, t):
                n = T * b + t
                if t == 0:
                    pe.wait_ge(qhi, b + 1)
                    pe.wait_ge(qlo, b + 1)
                if n >= 2:
                    pe.wait_ge(probs, n - 1)
                else:
                    pe.wait_ge(rows_ev, B)
                cs = slice(t * P, (t + 1) * P)
                product(s_ps[n % 2][:], (q_hi[:, b % 2, cs], q_lo[:, b % 2, cs]), (ht_hi[:, b % 2], ht_lo[:, b % 2])).then_inc(s_mm, 1)

            def p_transposes(b, t):
                n = T * b + t
                pe.wait_ge(probs, n + 1)
                if n >= 2:
                    pe.wait_ge(ptlo, n - 1)
                for k in range(T):
                    i = pe.transpose(t_ps[n % 2][:, k * P:(k + 1) * P], p_sb[:, t, k * P:(k + 1) * P], ident[:])
                i.then_inc(pt_mm, 1)

            def context(b):
                pe.wait_ge(hhi, b + 1)
                pe.wait_ge(hlo, b + 1)
                pe.wait_ge(ptlo, T * (b + 1))
                pe.wait_ge(pthi, T * (b + 1))
                if b:
                    pe.wait_ge(clo, b)
                for k in range(T):
                    i = product(c_ps[:], (h_hi[:, b % 2, k], h_lo[:, b % 2, k]), (pt_hi[:, k], pt_lo[:, k]),
                                start=(k == 0), stop=(k == T - 1))
                i.then_inc(c_mm, 1)

            def project_out(b):
                pe.wait_ge(chi, b + 1)
                pe.wait_ge(clo, b + 1)
                if b == 0:
                    pe.wait_ge(wv_split, 7)
                else:
                    pe.wait_ge(x1d, b)
                    pe.wait_ge(lmx, b)
                for t in range(T):
                    cs = slice(t * P, (t + 1) * P)
                    i = product(o_ps[:, t * D:(t + 1) * D], (ct_hi[:, cs], ct_lo[:, cs]), (wvg_hi[:, b], wvg_lo[:, b]))
                i.then_inc(o_mm, 1)

            def n2_transposes(b):
                pe.wait_ge(n2, b + 1)
                pe.wait_ge(htlo, min(b + 3, B))
                if b:
                    pe.wait_ge(h2d, b)
                for t in range(T):
                    i = pe.transpose(a_ps[:, t * P:(t + 1) * P], n2_sb[:, t], ident[:])
                i.then_inc(n2t_mm, 1)

            def router(b):
                pe.wait_ge(h2d, b + 1)
                pe.wait_ge(x1d, b + 1)
                for t in range(T):
                    i = pe.matmul(o_ps[:, t * E:(t + 1) * E], h2[:, b % 2, t * P:(t + 1) * P], router_w, start=True, stop=True)
                i.then_inc(l_mm, 1)

            def w_transposes(b):
                pe.wait_ge(wsd, b + 1)
                pe.wait_ge(qlo, min(b + 3, B))
                if b:
                    pe.wait_ge(wtd, b)
                for t in range(T):
                    i = pe.transpose(q_ps[0:KW, t * P:(t + 1) * P], full(wst[:, t]), ident[:])
                i.then_inc(wt_mm, 1)

            h_transposes(0)
            q_project(0)
            pe.wait_ge(htlo, 1)
            for m in range(3):
                i = pe.matmul(a_ps[:, m * B:(m + 1) * B], wmod[:, 3 + m], silu_c[:, :, 0], start=True, stop=True)
            i.then_inc(cols_mm, 1)
            for b in range(B):
                scores(b, 0)
                scores(b, 1)
                if b:
                    project_out(b - 1)
                scores(b, 2)
                p_transposes(b, 0)
                scores(b, 3)
                p_transposes(b, 1)
                if b + 1 < B:
                    h_transposes(b + 1)
                p_transposes(b, 2)
                if b + 1 < B:
                    q_project(b + 1)
                p_transposes(b, 3)
                if b:
                    n2_transposes(b - 1)
                    router(b - 1)
                context(b)
                if b:
                    w_transposes(b - 1)
            project_out(B - 1)

            def hidden(K):
                b, k = divmod(K, NK)
                e, c = divmod(k, HC)
                if k == 0:
                    pe.wait_ge(h2hi, b + 1)
                    pe.wait_ge(h2lo, b + 1)
                if b == 0 and c == 0:
                    pe.wait_ge(w_lo, e + 1)
                if K < 3:
                    pe.wait_ge(ptlo, T * B)
                    pe.wait_ge(probs, T * B)
                if K >= 3:
                    pe.wait_ge(gelu, K - 2)
                cs = slice(c * P, (c + 1) * P)
                product(hid_ps[K % 3][:], (w1_hi[:, e, cs], w1_lo[:, e, cs]), (h2_hi[:, b], h2_lo[:, b])).then_inc(hid_mm, 1)

            def spread_weights(b, e):
                n = b * E + e - 1
                if n == 0:
                    pe.wait_ge(h2d, B)
                pe.wait_ge(wtd, b + 1)
                if n == 0:
                    pe.wait_ge(picked, 1)
                if n >= 2:
                    pe.wait_ge(wtd_k, HC * (n - 1))
                pe.matmul(wb_ps[(n + 1) % 2][:], pick[:, e - 1], wt_t[:, b], start=True, stop=True).then_inc(wb_mm, 1)

            def accumulate(K):
                b, k = divmod(K, NK)
                e, c = divmod(k, HC)
                if K == 0:
                    pe.wait_ge(clo, B)
                if k == 0 and b == 1:
                    pe.wait_ge(lmx, B)
                    pe.wait_ge(x1d, B)
                if k == 0 and b >= 2:
                    pe.wait_ge(yev, b - 1)
                pe.wait_ge(thi, K + 1)
                pe.wait_ge(tlo, K + 1)
                cs = slice(c * D, (c + 1) * D)
                i = product(acc_ps[b % 2][:], (w2_hi[:, e, cs], w2_lo[:, e, cs]), (t_hi[:, K % SL], t_lo[:, K % SL]),
                            start=(k == 0), stop=False if k < NK - 1 else True)
                i.then_inc(acc_k, 1)

            def expert_bias(b):
                pe.wait_ge(wtd, b + 1)
                if b == 0:
                    pe.wait_ge(rb2_sem, 2)
                pe.matmul(acc_ps[b % 2][:], rb2_st[:], wt_t[:, b], start=False, stop=False)

            def y_transposes(b):
                pe.wait_ge(yev, b + 1)
                if b:
                    pe.wait_ge(outd, b)
                else:
                    pe.wait_ge(wtd, B)
                for t in range(T):
                    i = pe.transpose(y_ps[:, t * P:(t + 1) * P], y_sb[:, b % 2, t * P:(t + 1) * P], ident[:])
                i.then_inc(y_mm, 1)

            for K in range(3):
                hidden(K)
            n2_transposes(B - 1)
            router(B - 1)
            for K in range(B * NK):
                b, k = divmod(K, NK)
                n = K + 3
                if n < B * NK:
                    hidden(n)
                m = K + 2
                if m < B * NK and m % NK >= HC and m % HC == 0:
                    spread_weights(m // NK, (m % NK) // HC)
                accumulate(K)
                if K == 5:
                    w_transposes(B - 1)
                if k == 3:
                    expert_bias(b)
                if b and k == 5:
                    y_transposes(b - 1)
            y_transposes(B - 1)


def kernel(L0_attn_x, L0_attn_Wq, L0_attn_Wk, L0_attn_Wv, L0_ffn_router_w, L0_ffn_router_b, L0_ffn_sw1, L0_ffn_sb1,
           L0_ffn_sw2, L0_ffn_sb2, L0_ffn_rw1, L0_ffn_rb1, L0_ffn_rw2, L0_ffn_rb2, L0_c, L0_wmod):
    import numpy as np
    import concourse.bacc as bacc
    from concourse.bass_utils import run_bass_kernel_spmd

    f = lambda a: np.asarray(a)
    E, D, H = f(L0_ffn_rw1).shape
    hc = H // P
    w1 = np.concatenate([f(L0_ffn_sw1)[None], f(L0_ffn_rw1)]).transpose(1, 0, 2)
    w2 = np.concatenate([f(L0_ffn_sw2)[None], f(L0_ffn_rw2)]).reshape(E + 1, hc, P, D).transpose(2, 0, 1, 3)
    b1 = np.concatenate([f(L0_ffn_sb1)[None], f(L0_ffn_rb1)]).reshape(E + 1, hc, P).transpose(2, 0, 1)
    early = np.concatenate([f(L0_c).T, f(L0_wmod)], axis=1)
    late = np.concatenate([f(L0_attn_Wq), f(L0_attn_Wk), f(L0_attn_Wv).T, f(L0_ffn_router_w),
                           b1.reshape(P, -1), f(L0_ffn_sb2)[:, None]], axis=1)
    arrays = {
        "x": f(L0_attn_x), "early": early, "late": late, "router_b": f(L0_ffn_router_b)[None],
        "w1": w1, "w2": w2.reshape(P, E + 1, hc * D), "rb2": f(L0_ffn_rb2),
    }
    arrays = {k: np.ascontiguousarray(v) for k, v in arrays.items()}
    nc = bacc.Bacc("TRN2", target_bir_lowering=False, num_devices=1)
    args = [nc.dram_tensor(n, a.shape, mybir.dt.from_np(a.dtype), kind="ExternalInput").ap() for n, a in arrays.items()]
    out = nc.dram_tensor("out", arrays["x"].shape, F32, kind="ExternalOutput").ap()
    adaln_attention_moe(nc, *args, out)
    r = run_bass_kernel_spmd(nc, [arrays], core_ids=[0])
    return r.results[0]["out"]
```

```python
import concourse.bass as bass
from concourse import mybir
from contextlib import ExitStack
import math

F32 = mybir.dt.float32
F32R = mybir.dt.float32r
ALU = mybir.AluOpType
ACT = mybir.ActivationFunctionType
AX = mybir.AxisListType

P = 128
EPS = 1e-5


def adaln_attention_moe(nc, x, early, late, router_b, w1, w2, rb2, out):
    B, S, D = x.shape
    T = S // P
    E = rb2.shape[0]
    NE = E + 1
    HC = w1.shape[2] // P
    NK = NE * HC
    assert D == P and S == 512 and w1.shape[1] == NE
    SCALE = float(D) ** -0.5
    HB = 2
    HT = T // HB
    U = B * HB
    KW = 64 + E
    WHOLE = 96
    H2_LATE = ((B - 2, 4), (B - 1, 9))
    LOGITS_LATE = ((B - 3, 0), (B - 2, 7), (B - 1, 12))
    AHEAD = 4
    ROUTE_STEPS = 18
    ROUTE_AT = (6, 0)
    WT_AT = (13, 13)

    with ExitStack() as ctx:
        def sb(name, shape, dt=F32):
            return ctx.enter_context(nc.sbuf_tensor(name, shape, dt))

        def sem(name):
            return ctx.enter_context(nc.semaphore(name))

        def full(t):
            return t.bitcast(F32)

        early_sb = sb("early_sb", [P, early.shape[1]])
        late_sb = sb("late_sb", [P, late.shape[1]])
        c_t = early_sb[:, 0:B]
        wmod = early_sb[:, B:B + 6 * D].rearrange("p (m n) -> p m n", m=6)
        o = 0
        wq = late_sb[:, o:o + D]; o += D
        wk = late_sb[:, o:o + D]; o += D
        wv = late_sb[:, o:o + D]; o += D
        router_w = late_sb[:, o:o + E]; o += E
        b1 = late_sb[:, o:o + NK].rearrange("p (e c) -> p e c", c=HC); o += NK
        sb2 = late_sb[:, o:o + 1]
        rb_sb = sb("rb_sb", [P, E])
        rb2_sb = sb("rb2_sb", [KW, D])
        rb2_hi = sb("rb2_hi", [KW, D], F32R)
        rb2_st = sb("rb2_st", [KW, D], F32R)
        ident = sb("ident", [P, P])
        order = sb("order", [P, E])
        half = sb("half", [P, T])
        euler = sb("euler", [P, T, E])
        w1_sb = sb("w1_sb", [P, NE, HC * P])
        w1_hi = sb("w1_hi", [P, NE, HC * P], F32R)
        w1_lo = sb("w1_lo", [P, NE, HC * P], F32R)
        w2_sb = sb("w2_sb", [P, NE, HC * D])
        w2_hi = sb("w2_hi", [P, NE, HC * D], F32R)
        w2_lo = sb("w2_lo", [P, NE, HC * D], F32R)
        silu_e = sb("silu_e", [P, B])
        silu_d = sb("silu_d", [P, B])
        silu_r = sb("silu_r", [P, B])
        silu_s = sb("silu_s", [P, B])
        SA, CA, SB, CB, GA, GB = range(6)
        IN_WMOD = (0, 1, 3, 4, 2, 5)
        cols = sb("cols", [P, 6, B])
        ca1 = sb("ca1", [P, B])
        cb1 = sb("cb1", [P, B])
        g_sign = sb("g_sign", [P, 2, B])
        g_unit = sb("g_unit", [P, 2, B])
        g_abs = sb("g_abs", [P, 2, B])
        g_cols = sb("g_cols", [P, 2, B])
        ga, gb = g_cols[:, 0], g_cols[:, 1]
        gbb2 = sb("gbb2", [P, B])
        sa_c = sb("sa_c", [P, B, P])
        wv_ga = sb("wv_ga", [P, B, D])
        wvt_ga = sb("wvt_ga", [P, B, D])
        vrow = sa_c
        wvg = wv_ga
        wvg_hi = sb("wvg_hi", [P, B, D], F32R)
        wvg_lo = sb("wvg_lo", [P, B, D], F32R)
        g_f = sb("g_f", [P, D])
        g_hi = sb("g_hi", [P, D], F32R)
        g_lo = sb("g_lo", [P, D], F32R)
        x_sb = sb("x_sb", [P, B, T, D])
        x1_sb = sb("x1_sb", [P, B, T, D])
        stats = sb("stats", [P, 2, B, T, 6])
        mv = sb("mv", [P, 2, B, T, 2])
        ve = sb("ve", [P, 2, B, T])
        rstd = sb("rstd", [P, 2, B, T])
        nh_sb = sb("nh_sb", [P, 4, T, D])
        n_sb = nh_sb[:, 0:2]
        ht = nh_sb[:, 2].rearrange("p t d -> p (t d)")
        n_hi = sb("n_hi", [P, 2, T, D], F32R)
        n_lo = sb("n_lo", [P, 2, T, D], F32R)
        ht_hi = sb("ht_hi", [P, 2, S], F32R)
        ht_lo = sb("ht_lo", [P, 2, S], F32R)
        q_hi = sb("q_hi", [P, 2, S], F32R)
        q_lo = sb("q_lo", [P, 2, S], F32R)
        nmax = sb("nmax", [P, B, T])
        rsum = sb("rsum", [P, B, T])
        rinv = sb("rinv", [P, B, T])
        n_mid = sb("n_mid", [P, T, D])
        p_sb = sb("p_sb", [P, T, S])
        pt_hi = sb("pt_hi", [P, HB, T, HT * P], F32R)
        pt_lo = sb("pt_lo", [P, HB, T, HT * P], F32R)
        ct_hi = sb("ct_hi", [P, HT * P], F32R)
        ct_lo = sb("ct_lo", [P, HT * P], F32R)
        n2_sb = sb("n2_sb", [P, T, D])
        lg = sb("lg", [P, B, T, E])
        lmax = sb("lmax", [P, B, T])
        le = sb("le", [P, B, T, E])
        ex = sb("ex", [P, B, T, E])
        es = sb("es", [P, T])
        er = sb("er", [P, T])
        pr = sb("pr", [P, T, E])
        pr_left = sb("pr_left", [P, T, E])
        top = sb("top", [P, T])
        is_top = sb("is_top", [P, T, E])
        first_of = sb("first_of", [P, T])
        chosen = sb("chosen", [P, 2, T, E])
        wt = sb("wt", [P, T, E])
        wst = sb("wst", [P, T, WHOLE + E])
        wt_t = sb("wt_t", [KW, 2, S], F32R)
        wt_rows = sb("wt_rows", [WHOLE + E, 2, S])
        wb = sb("wb", [P, E, S])
        h2 = sb("h2", [P, 2, S])
        h2_hi = sb("h2_hi", [P, B, S], F32R)
        h2_lo = sb("h2_lo", [P, B, S], F32R)
        SL = 4
        act_sb = p_sb
        t_sb = nh_sb[:].rearrange("p a t d -> p a (t d)")
        t_hi = pt_hi[:].rearrange("p a k q -> p (a k q)").rearrange("p (a s) -> p a s", a=SL)
        t_lo = pt_lo[:].rearrange("p a k q -> p (a k q)").rearrange("p (a s) -> p a s", a=SL)
        out_sb = x_sb[:, 0:2]
        y_sb = x_sb[:, 2:4].rearrange("p b t d -> p b (t d)")

        bank = [ctx.enter_context(nc.psum_tensor(f"bank{i}", [P, 512], F32)) for i in range(8)]
        s_ps, t_ps = bank[0:2], bank[2:4]
        a_ps, q_ps, c_ps, o_ps = bank[4:8]
        hid_ps = bank[0:AHEAD]
        acc_ps = bank[6:8]

        early_in = sem("early_in"); x_in = [sem(f"x_in{b}") for b in range(B)]
        late_in = sem("late_in"); small_in = sem("small_in")
        w1_in = sem("w1_in"); w2_in = sem("w2_in"); stored = [sem(f"stored{i}") for i in range(2)]
        consts = sem("consts"); silu_exp = sem("silu_exp"); silu = sem("silu")
        cols_mm = sem("cols_mm"); cols_ev = sem("cols_ev"); colmod = sem("colmod"); gmod = sem("gmod")
        wv_mul = sem("wv_mul"); wvt_mm = sem("wvt_mm"); wvt_d = sem("wvt_d"); wvg_d = sem("wvg_d"); v_mm = sem("v_mm"); vrow_d = sem("vrow_d"); sac = sem("sac")
        g_mm = sem("g_mm"); g_split = sem("g_split"); wvg_h = sem("wvg_h"); wvg_l = sem("wvg_l")
        w_hi = sem("w_hi"); w_lo = sem("w_lo"); rb2_sem = sem("rb2_sem");
        st1 = sem("st1"); mv1 = sem("mv1"); ve1 = sem("ve1"); rs1 = sem("rs1"); nmid = sem("nmid"); n1 = sem("n1"); xr = sem("xr")
        nhi = sem("nhi"); nlo = sem("nlo"); nt_mm = sem("nt_mm"); htd = sem("htd"); hthi = sem("hthi"); htlo = sem("htlo")
        q_mm = sem("q_mm"); qhi = sem("qhi"); qlo = sem("qlo")
        s_mm = sem("s_mm"); nmx = sem("nmx"); probs = sem("probs"); pt_mm = sem("pt_mm"); pthi = sem("pthi"); ptlo = sem("ptlo")
        c_mm = sem("c_mm"); chi = sem("chi"); clo = sem("clo"); o_mm = sem("o_mm"); rinvd = sem("rinvd"); x1d = sem("x1d")
        st2 = sem("st2"); mv2 = sem("mv2"); ve2 = sem("ve2"); rs2 = sem("rs2"); n2 = sem("n2"); n2t_mm = sem("n2t_mm")
        h2d = sem("h2d"); h2hi = sem("h2hi"); h2lo = sem("h2lo")
        l_mm = sem("l_mm"); lgd = sem("lgd"); rt = sem("rt"); rexp = sem("rexp"); lmaxd = sem("lmaxd"); lmx = sem("lmx")
        wsd = sem("wsd"); wt_mm = sem("wt_mm"); wrows = sem("wrows"); wtd = sem("wtd")
        hid_mm = sem("hid_mm"); gelu = sem("gelu"); wb_in = [sem(f"wb_in{e}") for e in range(NE)]; wtd_k = sem("wtd_k"); thi = sem("thi"); tlo = sem("tlo")
        acc_k = sem("acc_k"); yev = sem("yev"); y_mm = sem("y_mm"); outd = sem("outd")

        block = ctx.enter_context(nc.Block())

        def weighed(K):
            b, k = divmod(K, NK)
            return b * (NK - HC) + max(0, k + 1 - HC)

        @block.sync
        def _(sp):
            def load_x(b):
                sp.dma_start(x_sb[:, b], x[b].rearrange("(p t) d -> p t d", t=T)).then_inc(x_in[b], 16)

            load_x(0)
            sp.dma_start(early_sb[:], early).then_inc(early_in, 16)
            sp.dma_start(late_sb[:], late).then_inc(late_in, 16)
            for b in range(1, B):
                load_x(b)
            sp.dma_start(w1_sb[:], w1).then_inc(w1_in, 16)
            sp.dma_start(w2_sb[:], w2).then_inc(w2_in, 16)
            sp.wait_ge(consts, 6)
            for q in (0, 32, 64):
                sp.dma_start(rb2_sb[q:q + E, :], rb2).then_inc(small_in, 16)
            sp.dma_start(rb_sb[:], router_b.to_broadcast([P, E])).then_inc(small_in, 16)

            def spread_weights(b):
                sp.wait_ge(wrows, b + 1)
                for e in range(1, NE):
                    if b:
                        sp.wait_ge(wtd_k, b * (NK - HC) - (NE - 1 - e) * HC)
                    sp.dma_start(wb[:, e - 1], wt_rows[WHOLE + e - 1:WHOLE + e, b % 2][:, None].to_broadcast([1, P, S])).then_inc(wb_in[e], 16)

            def store(b):
                sp.wait_ge(outd, b + 1)
                sp.dma_start(out[b].rearrange("(p t) d -> p t d", t=T), out_sb[:, b % 2]).then_inc(stored[b % 2], 16)

            for b in range(B):
                spread_weights(b)
                if b:
                    store(b - 1)
            store(B - 1)
            for i in range(2):
                sp.wait_ge(stored[i], 16 * ((B + 1 - i) // 2))

        @block.gpsimd
        def _(pool):
            pool.memset(half[:], -0.5).then_inc(consts, 1)
            pool.memset(ident[:], 0.0).then_inc(consts, 1)
            for e in range(E):
                i = pool.memset(order[:, e:e + 1], float(E - e))
            i.then_inc(consts, 1)
            pool.memset(wst[:], 0.0).then_inc(consts, 1)
            pool.memset(rb2_sb[:], 0.0).then_inc(consts, 1)
            pool.memset(euler[:], math.e).then_inc(consts, 1)
            pool.wait_ge(consts, 6)
            pool.affine_select(out=ident[:], in_=ident[:], compare_op=ALU.not_equal, fill=1.0, base=0,
                               pattern=[[-1, P]], channel_multiplier=1).then_inc(consts, 1)

            def rsqrt_var(n, b, ves, rss):
                pool.wait_ge(ves, b + 1)
                pool.tensor_tensor(rstd[:, n, b], ve[:, n, b], half[:], ALU.pow).then_inc(rss, 1)
                pool.wait_ge(rss, b + 1)

            def norm1(b):
                rsqrt_var(0, b, ve1, rs1)
                if b < 2:
                    return
                normalise(0, b, x_sb, (nt_mm, nhi, nlo), b - 1, n_sb[:, b % 2], n1)

            def normalise(n, b, src, readers, read, dst, done):
                pool.tensor_tensor(n_mid[:], src[:, b], mv[:, n, b, :, 0:1].to_broadcast([P, T, D]), ALU.subtract).then_inc(nmid, 1)
                pool.wait_ge(nmid, b - 1 if n == 0 else b + B - 1)
                for reader in readers:
                    pool.wait_ge(reader, read)
                pool.tensor_tensor(dst, n_mid[:], rstd[:, n, b, :, None].to_broadcast([P, T, D]), ALU.mult).then_inc(done, 1)

            def norm2(b):
                rsqrt_var(1, b, ve2, rs2)
                normalise(1, b, x1_sb, (n2t_mm,), b, n2_sb[:], n2)

            def n_split_lo(b):
                pool.wait_ge(nhi, b + 1)
                pool.wait_ge(n1, b + 1)
                if b >= 2:
                    pool.wait_ge(c_mm, HB * (b - 1))
                pool.tensor_tensor(n_lo[:, b % 2], n_sb[:, b % 2], full(n_hi[:, b % 2]), ALU.subtract).then_inc(nlo, 1)

            def add_vrow(b):
                pool.wait_ge(vrow_d, 1)
                pool.wait_ge(n1, b + 1)
                pool.tensor_tensor(x_sb[:, b], x_sb[:, b], vrow[:, b:b + 1].to_broadcast([P, T, D]), ALU.add).then_inc(xr, 1)

            def router_exp(b):
                pool.wait_ge(lmx, b + 1)
                pool.tensor_tensor(ex[:, b], euler[:], le[:, b], ALU.pow).then_inc(rexp, 1)

            def h2_split_lo(b):
                pool.wait_ge(h2hi, b + 1)
                pool.tensor_tensor(h2_lo[:, b], h2[:, b % 2], full(h2_hi[:, b]), ALU.subtract).then_inc(h2lo, 1)

            def weights_lo(e):
                pool.wait_ge(w_hi, e + 1)
                pool.tensor_tensor(w1_lo[:, e], w1_sb[:, e], full(w1_hi[:, e]), ALU.subtract)
                pool.tensor_tensor(w2_lo[:, e], w2_sb[:, e], full(w2_hi[:, e]), ALU.subtract).then_inc(w_lo, 1)

            norm1(0)
            norm1(1)
            n_split_lo(0)
            for u in range(U):
                b, first = u // HB, u % HB == 0
                if first and b:
                    add_vrow(b - 1)
                    n_split_lo(b)
                if u == U - 1:
                    h2_split_lo(0)
                if not first and b + 2 < B:
                    norm1(b + 2)
                if not first and b >= 2:
                    norm2(b - 2)
                if u >= 3:
                    for e in range(NE * (u - 3) // (U - 3), NE * (u - 2) // (U - 3)):
                        weights_lo(e)
            add_vrow(B - 1)
            norm2(B - 2)
            router_exp(1)
            norm2(B - 1)
            h2_split_lo(1)
            for b in range(2, B):
                h2_split_lo(b)
                router_exp(b)

        @block.scalar
        def _(act):
            act.wait_ge(early_in, 16)
            act.activation(silu_e[:], c_t, ACT.Exp, scale=-1.0).then_inc(silu_exp, 1)

            def n_split_hi(b):
                act.wait_ge(n1, b + 1)
                if b >= 2:
                    act.wait_ge(c_mm, HB * (b - 1))
                    act.wait_ge(nlo, b - 1)
                act.activation(n_hi[:, b % 2], n_sb[:, b % 2], ACT.Copy).then_inc(nhi, 1)

            def ht_make(b):
                act.wait_ge(nt_mm, b + 1)
                if b == 0:
                    act.wait_ge(colmod, 1)
                else:
                    act.wait_ge(htlo, b)
                    act.wait_ge(hthi, b)
                act.activation(ht, a_ps[:], ACT.Identity, scale=ca1[:, b:b + 1], bias=cols[:, SA, b:b + 1]).then_inc(htd, 1)
                act.wait_ge(htd, b + 1)
                if b >= 2:
                    act.wait_ge(s_mm, T * (b - 1))
                    act.wait_ge(htlo, b - 1)
                act.activation(ht_hi[:, b % 2], ht, ACT.Copy).then_inc(hthi, 1)

            def q_split_hi(b):
                act.wait_ge(q_mm, b + 1)
                if b >= 2:
                    act.wait_ge(s_mm, T * (b - 1))
                    act.wait_ge(qlo, b - 1)
                act.activation(q_hi[:, b % 2], q_ps[:], ACT.Copy).then_inc(qhi, 1)

            def exps(n):
                b, t = divmod(n, T)
                act.wait_ge(nmx, n + 1)
                if b:
                    act.wait_ge(pt_mm, n - T + 1)
                act.activation(p_sb[:, t], s_ps[n % 2][:], ACT.Exp, bias=nmax[:, b, t:t + 1],
                               accum_out=rsum[:, b, t:t + 1]).then_inc(probs, 1)

            def pt_split_hi(n):
                u, i = divmod(n, HT)
                act.wait_ge(pt_mm, n + 1)
                if u >= 2:
                    act.wait_ge(c_mm, u - 1)
                    act.wait_ge(ptlo, HT * (u - 1))
                act.activation(pt_hi[:, u % 2, :, i * P:(i + 1) * P], t_ps[n % 2][:].rearrange("p (k q) -> p k q", k=T),
                               ACT.Copy).then_inc(pthi, 1)

            def c_split_hi(u):
                act.wait_ge(c_mm, u + 1)
                if u:
                    act.wait_ge(o_mm, u)
                    act.wait_ge(clo, u)
                act.activation(ct_hi[:], c_ps[:, 0:HT * P], ACT.Copy).then_inc(chi, 1)

            def h2_make(b):
                act.wait_ge(n2t_mm, b + 1)
                act.wait_ge(colmod, 2)
                if b >= 2:
                    act.wait_ge(h2lo, b - 1)
                    act.wait_ge(l_mm, b - 1)
                act.activation(h2[:, b % 2], a_ps[:], ACT.Identity, scale=cb1[:, b:b + 1], bias=cols[:, SB, b:b + 1]).then_inc(h2d, 1)
                act.wait_ge(h2d, b + 1)
                act.activation(h2_hi[:, b], h2[:, b % 2], ACT.Copy).then_inc(h2hi, 1)

            def weights_hi(e):
                if e == 0:
                    act.wait_ge(w1_in, 16)
                    act.wait_ge(w2_in, 16)
                act.activation(w1_hi[:, e], w1_sb[:, e], ACT.Copy)
                act.activation(w2_hi[:, e], w2_sb[:, e], ACT.Copy).then_inc(w_hi, 1)

            def router_exp(b):
                act.wait_ge(lmx, b + 1)
                act.activation(ex[:, b], le[:, b], ACT.Exp).then_inc(rexp, 1)

            ht_make(0)
            n_split_hi(0)
            q_split_hi(0)
            ht_make(1)
            act.wait_ge(gmod, 4)
            for b in range(B):
                i = act.activation(wv_ga[:, b], wv, ACT.Identity, scale=ga[:, b:b + 1])
            i.then_inc(wv_mul, 1)
            for u in range(U + 1):
                b, first = u // HB, u % HB == 0
                for i in range(HT):
                    if i == 1 and not first and b + 1 < B:
                        q_split_hi(b + 1)
                    if u:
                        pt_split_hi(HT * (u - 1) + i)
                    if u < U:
                        exps(HT * u + i)
                    if i == 0 and first and 0 < b < B - 1:
                        ht_make(b + 1)
                    if i == 0 and first and 0 < b < B:
                        n_split_hi(b)
                    if i == 1 and u == U - 2:
                        h2_make(0)
                    if i == 0 and u == U - 1:
                        router_exp(0)
                if u >= 2:
                    c_split_hi(u - 2)
                if u == 0:
                    act.wait_ge(wvt_mm, 1)
                    act.activation(wvt_ga[:], o_ps[:].rearrange("p (b d) -> p b d", b=B), ACT.Copy).then_inc(wvt_d, 1)
                if u == 1:
                    act.wait_ge(wvt_d, 1)
                    for n in range(B):
                        i = act.activation(wvg[:, n], wvt_ga[:, n], ACT.Identity, scale=ca1[:, n:n + 1])
                    i.then_inc(wvg_d, 1)
                    act.wait_ge(v_mm, 1)
                    act.activation(vrow[:], c_ps[:].rearrange("p (b d) -> p b d", b=B), ACT.Copy).then_inc(vrow_d, 1)
                    act.wait_ge(wvg_d, 1)
                    act.activation(wvg_hi[:], wvg[:], ACT.Copy).then_inc(wvg_h, 1)
                if 2 <= u < U:
                    for e in range(NE * (u - 2) // (U - 2), NE * (u - 1) // (U - 2)):
                        weights_hi(e)

            def gelus(K):
                b, k = divmod(K, NK)
                act.wait_ge(hid_mm, K + 1)
                if K >= SL:
                    if (K - SL) % NK < HC:
                        act.wait_ge(thi, K - SL + 1)
                        act.wait_ge(tlo, K - SL + 1)
                    else:
                        act.wait_ge(wtd_k, weighed(K - SL))
                act.activation(act_sb[:, K % SL], hid_ps[K % AHEAD][:], ACT.Gelu, bias=b1[:, k // HC, k % HC:k % HC + 1]).then_inc(gelu, 1)

            def split_hi(K):
                k = K % NK
                if k < HC:
                    act.wait_ge(gelu, K + 1)
                else:
                    act.wait_ge(wtd_k, weighed(K))
                if K % 2 == 0 and K < SL:
                    act.wait_ge(c_mm, U - 1 + K // 2)
                if K >= SL:
                    act.wait_ge(acc_k, K - SL + 1)
                    act.wait_ge(tlo, K - SL + 1)
                src = act_sb if k < HC else t_sb
                act.activation(t_hi[:, K % SL], src[:, K % SL], ACT.Copy).then_inc(thi, 1)

            def weight_rows(b):
                act.wait_ge(wt_mm, b + 1)
                if b >= 2:
                    for e in range(1, NE):
                        act.wait_ge(wb_in[e], 16 * (b - 1))
                act.activation(wt_rows[WHOLE:, b % 2], a_ps[WHOLE:WHOLE + E, :], ACT.Copy).then_inc(wrows, 1)

            def y_evac(b):
                act.wait_ge(acc_k, (b + 1) * NK)
                if b >= 2:
                    act.wait_ge(y_mm, b - 1)
                act.activation(y_sb[:, b % 2], acc_ps[b % 2][:], ACT.Identity, scale=gb[:, b:b + 1],
                               bias=gbb2[:, b:b + 1]).then_inc(yev, 1)

            gelus(0)
            h2_make(1)
            gelus(1)
            c_split_hi(U - 1)
            for K in range(B * NK):
                b, k = divmod(K, NK)
                if 2 <= K + 1 < B * NK:
                    gelus(K + 1)
                for late, when in H2_LATE:
                    if K == when + 2:
                        h2_make(late)
                split_hi(K)
                if K == 0:
                    weight_rows(0)
                if b + 1 < B and k == WT_AT[b > 0] + 2:
                    weight_rows(b + 1)
                if b and k == 2:
                    y_evac(b - 1)
            y_evac(B - 1)

        @block.vector
        def _(dve):
            def layer_stats(n, b, src, sts, t0, t1):
                for t in range(t0, t1):
                    i = dve.bn_stats(stats[:, n, b, t], src[:, b, t])
                i.then_inc(sts, 1)

            def layer_mean_var(n, b, sts, mvs, ves):
                dve.wait_ge(sts, (b + 1) * (1 if n == 0 else HB))
                for t in range(T):
                    i = dve.bn_aggr(mv[:, n, b, t], stats[:, n, b, t])
                i.then_inc(mvs, 1)
                dve.wait_ge(mvs, b + 1)
                dve.tensor_scalar(ve[:, n, b], mv[:, n, b, :, 1], EPS, None, ALU.add).then_inc(ves, 1)

            def stats1(b):
                dve.wait_ge(x_in[b], 16)
                layer_stats(0, b, x_sb, st1, 0, T)
                layer_mean_var(0, b, st1, mv1, ve1)

            def norm(n, b, dst, src, rss, done):
                dve.wait_ge(rss, b + 1)
                for t in range(T):
                    i = dve.tensor_scalar(dst[:, t], src[:, b, t], mv[:, n, b, t, 0:1], rstd[:, n, b, t:t + 1],
                                          ALU.subtract, ALU.mult)
                i.then_inc(done, 1)

            def ht_split_lo(b):
                dve.wait_ge(hthi, b + 1)
                if b >= 2:
                    dve.wait_ge(s_mm, T * (b - 1))
                dve.tensor_tensor(ht_lo[:, b % 2], ht, full(ht_hi[:, b % 2]), ALU.subtract).then_inc(htlo, 1)

            def q_split_lo(b):
                dve.wait_ge(qhi, b + 1)
                if b >= 2:
                    dve.wait_ge(s_mm, T * (b - 1))
                dve.tensor_tensor(q_lo[:, b % 2], q_ps[:], full(q_hi[:, b % 2]), ALU.subtract).then_inc(qlo, 1)

            def row_max(n):
                dve.wait_ge(s_mm, n + 1)
                dve.tensor_reduce(nmax[:, n // T, n % T:n % T + 1], s_ps[n % 2][:], AX.X, ALU.max, negate=True).then_inc(nmx, 1)

            def pt_split_lo(n):
                u, i = divmod(n, HT)
                dve.wait_ge(pthi, n + 1)
                if u >= 2:
                    dve.wait_ge(c_mm, u - 1)
                dve.tensor_tensor(pt_lo[:, u % 2, :, i * P:(i + 1) * P], t_ps[n % 2][:].rearrange("p (k q) -> p k q", k=T),
                                  full(pt_hi[:, u % 2, :, i * P:(i + 1) * P]), ALU.subtract).then_inc(ptlo, 1)

            def c_split_lo(u):
                dve.wait_ge(chi, u + 1)
                if u:
                    dve.wait_ge(o_mm, u)
                dve.tensor_tensor(ct_lo[:], c_ps[:, 0:HT * P], full(ct_hi[:]), ALU.subtract).then_inc(clo, 1)

            def row_sums(u):
                b, t0 = u // HB, HT * (u % HB)
                dve.wait_ge(probs, HT * (u + 1))
                dve.reciprocal(rinv[:, b, t0:t0 + HT], rsum[:, b, t0:t0 + HT]).then_inc(rinvd, 1)

            def residual(u):
                b, t0 = u // HB, HT * (u % HB)
                dve.wait_ge(rinvd, u + 1)
                dve.wait_ge(o_mm, u + 1)
                dve.wait_ge(xr, b + 1)
                for t in range(t0, t0 + HT):
                    i = dve.scalar_tensor_tensor(x1_sb[:, b, t], o_ps[:, (t - t0) * D:(t - t0 + 1) * D], rinv[:, b, t:t + 1],
                                                 x_sb[:, b, t], ALU.mult, ALU.add)
                i.then_inc(x1d, 1)

            def stats2(u):
                b, t0 = u // HB, HT * (u % HB)
                dve.wait_ge(x1d, u + 1)
                layer_stats(1, b, x1_sb, st2, t0, t0 + HT)
                if u % HB == HB - 1:
                    layer_mean_var(1, b, st2, mv2, ve2)

            def router_logits(b):
                dve.wait_ge(l_mm, b + 1)
                if b == 0:
                    dve.wait_ge(small_in, 64)
                dve.tensor_tensor(lg[:, b], (o_ps if b else q_ps)[:, 0:T * E].rearrange("p (t e) -> p t e", t=T),
                                  rb_sb[:, None, :].to_broadcast([P, T, E]), ALU.add).then_inc(lgd, 1)
                dve.wait_ge(lgd, b + 1)
                dve.tensor_reduce(lmax[:, b], lg[:, b], AX.X, ALU.max).then_inc(lmaxd, 1)
                dve.wait_ge(lmaxd, b + 1)
                dve.tensor_tensor(le[:, b], lg[:, b], lmax[:, b, :, None].to_broadcast([P, T, E]), ALU.subtract).then_inc(lmx, 1)

            def router_steps(b):
                count = [ROUTE_STEPS * b]

                def step(make, *args):
                    if count[0]:
                        dve.wait_ge(rt, count[0])
                    make(*args).then_inc(rt, 1)
                    count[0] += 1

                def by_token(a):
                    return a[:, :, None].to_broadcast([P, T, E])

                dve.wait_ge(rexp, b + 1)
                step(dve.tensor_reduce, es[:], ex[:, b], AX.X, ALU.add)
                yield
                step(dve.reciprocal, er[:], es[:])
                yield
                step(dve.tensor_tensor, pr[:], ex[:, b], by_token(er), ALU.mult)
                yield
                for n, left in enumerate((pr, pr_left)):
                    step(dve.tensor_reduce, top[:], left[:], AX.X, ALU.max)
                    yield
                    step(dve.tensor_tensor, is_top[:], left[:], by_token(top), ALU.is_ge)
                    yield
                    step(dve.tensor_tensor, is_top[:], is_top[:], order[:, None].to_broadcast([P, T, E]), ALU.mult)
                    yield
                    step(dve.tensor_reduce, first_of[:], is_top[:], AX.X, ALU.max)
                    yield
                    step(dve.tensor_tensor, chosen[:, n], is_top[:], by_token(first_of), ALU.is_equal)
                    yield
                    if n == 0:
                        step(dve.scalar_tensor_tensor, pr_left[:], chosen[:, 0], -2.0, pr[:], ALU.mult, ALU.add)
                        yield
                step(dve.tensor_tensor, chosen[:, 0], chosen[:, 0], chosen[:, 1], ALU.add)
                yield
                step(dve.tensor_tensor, wt[:], chosen[:, 0], pr[:], ALU.mult)
                yield
                if b:
                    dve.wait_ge(wt_mm, b)
                step(dve.tensor_copy, wst[:, :, 0:E].bitcast(F32R), wt[:])
                yield
                dve.tensor_copy(wst[:, :, 64:64 + E].bitcast(F32R), wt[:])
                step(dve.tensor_copy, wst[:, :, WHOLE:WHOLE + E], wt[:])
                assert count[0] == ROUTE_STEPS * (b + 1)
                dve.tensor_tensor(wst[:, :, 32:32 + E].bitcast(F32R), wt[:], wst[:, :, 0:E], ALU.subtract).then_inc(wsd, 1)
                yield

            def weights_t(b):
                dve.wait_ge(wrows, b + 1)
                if b >= 2:
                    dve.wait_ge(acc_k, (b - 1) * NK)
                dve.tensor_copy(wt_t[:, b % 2], a_ps[0:KW, :]).then_inc(wtd, 1)

            stats1(0)
            dve.wait_ge(silu_exp, 1)
            dve.tensor_scalar(silu_d[:], silu_e[:], 1.0, None, ALU.add).then_inc(silu, 1)
            dve.wait_ge(silu, 1)
            dve.reciprocal(silu_r[:], silu_d[:]).then_inc(silu, 1)
            dve.wait_ge(silu, 2)
            dve.tensor_tensor(silu_s[:], silu_r[:], c_t, ALU.mult).then_inc(silu, 1)
            norm(0, 0, n_sb[:, 0], x_sb, rs1, n1)
            dve.wait_ge(cols_mm, 1)
            dve.tensor_copy(cols[:, SA:CA + 1], t_ps[0][:, 0:2 * B].rearrange("p (m b) -> p m b", m=2)).then_inc(cols_ev, 1)
            dve.wait_ge(cols_ev, 1)
            dve.tensor_scalar(ca1[:], cols[:, CA], 1.0, None, ALU.add).then_inc(colmod, 1)
            stats1(1)
            dve.wait_ge(g_mm, 1)
            dve.tensor_scalar(g_f[:], q_ps[:, 0:D], SCALE, None, ALU.mult).then_inc(g_split, 1)
            dve.wait_ge(g_split, 1)
            dve.tensor_copy(g_hi[:], g_f[:]).then_inc(g_split, 1)
            dve.wait_ge(g_split, 2)
            dve.tensor_tensor(g_lo[:], g_f[:], full(g_hi[:]), ALU.subtract).then_inc(g_split, 1)
            ht_split_lo(0)
            dve.tensor_copy(sa_c[:], cols[:, SA, :, None].to_broadcast([P, B, P])).then_inc(sac, 1)
            norm(0, 1, n_sb[:, 1], x_sb, rs1, n1)
            q_split_lo(0)
            stats1(2)
            dve.wait_ge(cols_mm, 2)
            dve.tensor_copy(cols[:, SB:GB + 1], t_ps[1][:, 0:4 * B].rearrange("p (m b) -> p m b", m=4)).then_inc(cols_ev, 1)
            dve.wait_ge(cols_ev, 2)
            dve.tensor_scalar(g_sign[:], cols[:, GA:GB + 1], 0.0, 2.0, ALU.is_ge, ALU.mult).then_inc(gmod, 1)
            dve.tensor_scalar(cb1[:], cols[:, CB], 1.0, None, ALU.add).then_inc(colmod, 1)
            dve.wait_ge(gmod, 1)
            dve.tensor_scalar(g_unit[:], g_sign[:], -1.0, None, ALU.add).then_inc(gmod, 1)
            dve.wait_ge(gmod, 2)
            dve.tensor_tensor(g_abs[:], g_unit[:], cols[:, GA:GB + 1], ALU.mult).then_inc(gmod, 1)
            dve.wait_ge(gmod, 3)
            dve.scalar_tensor_tensor(g_cols[:], g_abs[:], 0.25, g_unit[:], ALU.max, ALU.mult).then_inc(gmod, 1)
            ht_split_lo(1)
            dve.wait_ge(gmod, 4)
            dve.tensor_scalar(gbb2[:], gb, sb2, None, ALU.mult).then_inc(gmod, 1)

            def set_up(u):
                if u == 2:
                    dve.wait_ge(wvg_h, 1)
                    dve.tensor_tensor(wvg_lo[:], wvg[:], full(wvg_hi[:]), ALU.subtract).then_inc(wvg_l, 1)
                if u == 5:
                    dve.wait_ge(small_in, 64)
                    dve.tensor_copy(rb2_hi[:], rb2_sb[:]).then_inc(rb2_sem, 1)
                    dve.wait_ge(rb2_sem, 1)
                    dve.tensor_copy(rb2_st[0:64], full(rb2_hi[0:64]))
                    dve.tensor_tensor(rb2_st[64:KW], rb2_sb[64:KW], full(rb2_hi[64:KW]), ALU.subtract).then_inc(rb2_sem, 1)

            route = router_steps(0)

            def aside(u):
                if u >= U - 1:
                    next(route)

            for u in range(U + 1):
                b, first = u // HB, u % HB == 0
                if u < U:
                    row_max(HT * u)
                    if u == U - 1:
                        router_logits(0)
                    if u >= 3:
                        row_sums(u - 3)
                    row_max(HT * u + 1)
                else:
                    row_sums(u - 3)
                if u:
                    pt_split_lo(HT * (u - 1))
                    aside(u)
                    if first and b < B - 1:
                        ht_split_lo(b + 1)
                    if not first and b + 1 < B:
                        q_split_lo(b + 1)
                    pt_split_lo(HT * (u - 1) + 1)
                    aside(u)
                if u >= 3:
                    residual(u - 3)
                    aside(u)
                if u >= 2:
                    c_split_lo(u - 2)
                    aside(u)
                if u >= 3:
                    stats2(u - 3)
                if not first and b + 3 < B:
                    stats1(b + 3)
                if u < U:
                    set_up(u)
                aside(u)
            row_sums(U - 2)
            aside(U)
            row_sums(U - 1)
            aside(U)
            residual(U - 2)
            aside(U)
            for _ in route:
                pass
            c_split_lo(U - 1)
            residual(U - 1)

            def weigh(K):
                b, k = divmod(K, NK)
                if k < HC:
                    return
                e = k // HC
                dve.wait_ge(gelu, K + 1)
                dve.wait_ge(wb_in[e], 16 * (b + 1))
                if K >= SL:
                    dve.wait_ge(thi, K - SL + 1)
                    dve.wait_ge(tlo, K - SL + 1)
                dve.tensor_tensor(t_sb[:, K % SL], act_sb[:, K % SL], wb[:, e - 1], ALU.mult).then_inc(wtd_k, 1)

            def split_lo(K):
                k = K % NK
                dve.wait_ge(thi, K + 1)
                if K >= SL:
                    dve.wait_ge(acc_k, K - SL + 1)
                src = act_sb if k < HC else t_sb
                dve.tensor_tensor(t_lo[:, K % SL], src[:, K % SL], full(t_hi[:, K % SL]), ALU.subtract).then_inc(tlo, 1)

            def output(b):
                dve.wait_ge(y_mm, b + 1)
                if b >= 2:
                    dve.wait_ge(stored[b % 2], 16 * (b // 2))
                dve.tensor_tensor(out_sb[:, b % 2].rearrange("p t d -> p (t d)"), a_ps[:],
                                  x1_sb[:, b].rearrange("p t d -> p (t d)"), ALU.add).then_inc(outd, 1)

            for K in range(B * NK):
                b, k = divmod(K, NK)
                if K == HC - 1:
                    split_lo(K)
                    stats2(U - 2)
                    stats2(U - 1)
                if K + 1 < B * NK:
                    weigh(K + 1)
                if b + 1 < B:
                    if k == ROUTE_AT[b > 0]:
                        route = router_steps(b + 1)
                    if k >= ROUTE_AT[b > 0]:
                        next(route, None)
                if K != HC - 1:
                    split_lo(K)
                if K == HC:
                    weights_t(0)
                for late, when in LOGITS_LATE:
                    if K == when + 1:
                        router_logits(late)
                if b + 1 < B:
                    if k >= ROUTE_AT[b > 0] and (b == 0 or k < 5):
                        next(route, None)
                    if b == 0 and k >= ROUTE_AT[0] + 3:
                        next(route, None)
                    if k == WT_AT[b > 0] + 3:
                        weights_t(b + 1)
                if b and k == 6:
                    output(b - 1)
            output(B - 1)

        @block.tensor
        def _(pe):
            def product(ps, lhs, rhs, start=True, stop=True):
                pe.matmul(ps, lhs[0], rhs[0], start=start, stop=False)
                pe.matmul(ps, lhs[0], rhs[1], start=False, stop=False)
                return pe.matmul(ps, lhs[1], rhs[0], start=False, stop=stop)

            def n_transposes(b):
                pe.wait_ge(n1, b + 1)
                if b == 0:
                    pe.wait_ge(consts, 7)
                else:
                    pe.wait_ge(htd, b)
                for t in range(T):
                    i = pe.transpose(a_ps[:, t * P:(t + 1) * P], n_sb[:, b % 2, t], ident[:])
                i.then_inc(nt_mm, 1)

            def q_project(b):
                pe.wait_ge(hthi, b + 1)
                pe.wait_ge(htlo, b + 1)
                if b == 0:
                    pe.wait_ge(g_split, 3)
                else:
                    pe.wait_ge(qlo, b)
                product(q_ps[:], (g_hi[:], g_lo[:]), (ht_hi[:, b % 2], ht_lo[:, b % 2])).then_inc(q_mm, 1)

            def scores(n):
                b, t = divmod(n, T)
                if t == 0:
                    pe.wait_ge(qhi, b + 1)
                    pe.wait_ge(qlo, b + 1)
                if n >= 2:
                    pe.wait_ge(probs, n - 1)
                cs = slice(t * P, (t + 1) * P)
                product(s_ps[n % 2][:], (q_hi[:, b % 2, cs], q_lo[:, b % 2, cs]), (ht_hi[:, b % 2], ht_lo[:, b % 2])).then_inc(s_mm, 1)

            def p_transposes(n):
                pe.wait_ge(probs, n + 1)
                if n >= 2:
                    pe.wait_ge(ptlo, n - 1)
                else:
                    pe.wait_ge(cols_ev, n + 1)
                for k in range(T):
                    i = pe.transpose(t_ps[n % 2][:, k * P:(k + 1) * P], p_sb[:, n % T, k * P:(k + 1) * P], ident[:])
                i.then_inc(pt_mm, 1)

            def context(u):
                b = u // HB
                pe.wait_ge(nhi, b + 1)
                pe.wait_ge(nlo, b + 1)
                pe.wait_ge(ptlo, HT * (u + 1))
                if u:
                    pe.wait_ge(clo, u)
                else:
                    pe.wait_ge(vrow_d, 1)
                for k in range(T):
                    i = product(c_ps[:, 0:HT * P], (n_hi[:, b % 2, k], n_lo[:, b % 2, k]), (pt_hi[:, u % 2, k], pt_lo[:, u % 2, k]),
                                start=(k == 0), stop=(k == T - 1))
                i.then_inc(c_mm, 1)

            def project_out(u):
                b = u // HB
                pe.wait_ge(clo, u + 1)
                if u == 0:
                    pe.wait_ge(wvg_l, 1)
                else:
                    pe.wait_ge(x1d, u)
                for t in range(HT):
                    cs = slice(t * P, (t + 1) * P)
                    i = product(o_ps[:, t * D:(t + 1) * D], (ct_hi[:, cs], ct_lo[:, cs]), (wvg_hi[:, b], wvg_lo[:, b]))
                i.then_inc(o_mm, 1)

            def n2_transposes(b):
                pe.wait_ge(n2, b + 1)
                pe.wait_ge(htd, B)
                if b:
                    pe.wait_ge(h2d, b)
                if b >= 2:
                    pe.wait_ge(wtd, 1)
                for t in range(T):
                    i = pe.transpose(a_ps[:, t * P:(t + 1) * P], n2_sb[:, t], ident[:])
                i.then_inc(n2t_mm, 1)

            def router(b):
                pe.wait_ge(h2d, b + 1)
                if b == 0:
                    pe.wait_ge(qlo, B)
                if b:
                    pe.wait_ge(x1d, U)
                    pe.wait_ge(lgd, b)
                for t in range(T):
                    i = pe.matmul((o_ps if b else q_ps)[:, t * E:(t + 1) * E], h2[:, b % 2, t * P:(t + 1) * P], router_w, start=True, stop=True)
                i.then_inc(l_mm, 1)

            def w_transposes(b):
                pe.wait_ge(wsd, b + 1)
                pe.wait_ge(h2d, B - 2 if b == 0 else B)
                if b:
                    pe.wait_ge(wtd, b)
                if b >= 2:
                    pe.wait_ge(outd, b - 1)
                for t in range(T):
                    i = pe.transpose(a_ps[0:WHOLE + E, t * P:(t + 1) * P], wst[:, t], ident[:])
                i.then_inc(wt_mm, 1)

            def modulation(ps, parts):
                for n, m in enumerate(parts):
                    i = pe.matmul(ps[:, n * B:(n + 1) * B], wmod[:, IN_WMOD[m]], silu_s[:], start=True, stop=True)
                i.then_inc(cols_mm, 1)

            pe.wait_ge(silu, 3)
            modulation(t_ps[0], (SA, CA))
            n_transposes(0)
            pe.wait_ge(late_in, 16)
            pe.matmul(q_ps[:, 0:D], wq, wk, start=True, stop=True).then_inc(g_mm, 1)
            modulation(t_ps[1], (SB, CB, GA, GB))
            q_project(0)
            n_transposes(1)
            for u in range(U + 1):
                b, first = u // HB, u % HB == 0
                for i in range(HT):
                    if u < U:
                        scores(HT * u + i)
                    if i == 0 and first and 0 < b < B - 1:
                        n_transposes(b + 1)
                    if u:
                        p_transposes(HT * (u - 1) + i)
                    if i == 0 and not first and b + 1 < B:
                        q_project(b + 1)
                    if i == 0 and u == U - 2:
                        n2_transposes(0)
                if u == 0:
                    pe.wait_ge(wv_mul, 1)
                    for n in range(B):
                        i = pe.transpose(o_ps[:, n * D:(n + 1) * D], wv_ga[:, n], ident[:])
                    i.then_inc(wvt_mm, 1)
                if u == 1:
                    pe.wait_ge(wvt_d, 1)
                    for n in range(B):
                        i = pe.matmul(c_ps[:, n * D:(n + 1) * D], sa_c[:, n], wvt_ga[:, n], start=True, stop=True)
                    i.then_inc(v_mm, 1)
                if u >= 3:
                    project_out(u - 3)
                if u >= 2:
                    context(u - 2)
                if u == U - 2:
                    router(0)

            def hidden(K):
                b, k = divmod(K, NK)
                e, c = divmod(k, HC)
                if k == 0:
                    pe.wait_ge(h2hi, b + 1)
                    pe.wait_ge(h2lo, b + 1)
                if b == 0 and c == 0:
                    pe.wait_ge(w_lo, e + 1)
                if K < 2:
                    pe.wait_ge(probs, T * B - 1 + K)
                elif K < AHEAD:
                    pe.wait_ge(ptlo, T * B - 3 + K)
                else:
                    pe.wait_ge(gelu, K - AHEAD + 1)
                cs = slice(c * P, (c + 1) * P)
                product(hid_ps[K % AHEAD][:], (w1_hi[:, e, cs], w1_lo[:, e, cs]), (h2_hi[:, b], h2_lo[:, b])).then_inc(hid_mm, 1)

            def accumulate(K):
                b, k = divmod(K, NK)
                e, c = divmod(k, HC)
                if K == 0:
                    pe.wait_ge(clo, U)
                if k == 0 and b == 1:
                    pe.wait_ge(lgd, B)
                if k == 0 and b >= 2:
                    pe.wait_ge(yev, b - 1)
                pe.wait_ge(thi, K + 1)
                pe.wait_ge(tlo, K + 1)
                cs = slice(c * D, (c + 1) * D)
                i = product(acc_ps[b % 2][:], (w2_hi[:, e, cs], w2_lo[:, e, cs]), (t_hi[:, K % SL], t_lo[:, K % SL]),
                            start=(k == 0), stop=(k == NK - 1))
                i.then_inc(acc_k, 1)

            def expert_bias(b):
                pe.wait_ge(wtd, b + 1)
                if b == 0:
                    pe.wait_ge(rb2_sem, 2)
                pe.matmul(acc_ps[b % 2][:], rb2_st[:], wt_t[:, b % 2], start=False, stop=False)

            def y_transposes(b):
                pe.wait_ge(yev, b + 1)
                pe.wait_ge(wtd, min(b + 2, B))
                if b:
                    pe.wait_ge(outd, b)
                for t in range(T):
                    i = pe.transpose(a_ps[:, t * P:(t + 1) * P], y_sb[:, b % 2, t * P:(t + 1) * P], ident[:])
                i.then_inc(y_mm, 1)

            hidden(0)
            n2_transposes(1)
            hidden(1)
            project_out(U - 2)
            context(U - 1)
            hidden(2)
            w_transposes(0)
            project_out(U - 1)
            hidden(3)
            for K in range(B * NK):
                b, k = divmod(K, NK)
                n = K + AHEAD
                if n < B * NK:
                    hidden(n)
                if b + 1 < B and k == WT_AT[b > 0]:
                    w_transposes(b + 1)
                for late, when in H2_LATE:
                    if K == when:
                        n2_transposes(late)
                for late, when in LOGITS_LATE:
                    if K == when:
                        router(late)
                accumulate(K)
                if k == 3:
                    expert_bias(b)
                if b and k == 4:
                    y_transposes(b - 1)
            y_transposes(B - 1)


def kernel(L0_attn_x, L0_attn_Wq, L0_attn_Wk, L0_attn_Wv, L0_ffn_router_w, L0_ffn_router_b, L0_ffn_sw1, L0_ffn_sb1,
           L0_ffn_sw2, L0_ffn_sb2, L0_ffn_rw1, L0_ffn_rb1, L0_ffn_rw2, L0_ffn_rb2, L0_c, L0_wmod):
    import numpy as np
    import concourse.bacc as bacc
    from concourse.bass_utils import run_bass_kernel_spmd

    f = lambda a: np.asarray(a)
    E, D, H = f(L0_ffn_rw1).shape
    hc = H // P
    w1 = np.concatenate([f(L0_ffn_sw1)[None], f(L0_ffn_rw1)]).transpose(1, 0, 2)
    w2 = np.concatenate([f(L0_ffn_sw2)[None], f(L0_ffn_rw2)]).reshape(E + 1, hc, P, D).transpose(2, 0, 1, 3)
    b1 = np.concatenate([f(L0_ffn_sb1)[None], f(L0_ffn_rb1)]).reshape(E + 1, hc, P).transpose(2, 0, 1)
    early = np.concatenate([f(L0_c).T, f(L0_wmod)], axis=1)
    late = np.concatenate([f(L0_attn_Wq), f(L0_attn_Wk), f(L0_attn_Wv), f(L0_ffn_router_w),
                           b1.reshape(P, -1), f(L0_ffn_sb2)[:, None]], axis=1)
    arrays = {
        "x": f(L0_attn_x), "early": early, "late": late, "router_b": f(L0_ffn_router_b)[None],
        "w1": w1, "w2": w2.reshape(P, E + 1, hc * D), "rb2": f(L0_ffn_rb2),
    }
    arrays = {k: np.ascontiguousarray(v) for k, v in arrays.items()}
    nc = bacc.Bacc("TRN2", target_bir_lowering=False, num_devices=1)
    args = [nc.dram_tensor(n, a.shape, mybir.dt.from_np(a.dtype), kind="ExternalInput").ap() for n, a in arrays.items()]
    out = nc.dram_tensor("out", arrays["x"].shape, F32, kind="ExternalOutput").ap()
    adaln_attention_moe(nc, *args, out)
    r = run_bass_kernel_spmd(nc, [arrays], core_ids=[0])
    return r.results[0]["out"]
```

```python
import concourse.bass as bass
from concourse import mybir
from contextlib import ExitStack
import math

F32 = mybir.dt.float32
F32R = mybir.dt.float32r
ALU = mybir.AluOpType
ACT = mybir.ActivationFunctionType
AX = mybir.AxisListType

P = 128
EPS = 1e-5


def adaln_attention_moe(nc, x, early, late, router_b, w1, w2, rb2, out):
    B, S, D = x.shape
    T = S // P
    E = rb2.shape[0]
    NE = E + 1
    HC = w1.shape[2] // P
    NK = NE * HC
    assert D == P and S == 512 and w1.shape[1] == NE
    SCALE = float(D) ** -0.5
    HB = 2
    HT = T // HB
    U = B * HB
    KW = 64 + E
    WHOLE = 96
    H2_LATE = ((B - 2, 3), (B - 1, 9))
    LOGITS_LATE = ((B - 3, 0), (B - 2, 5), (B - 1, 12))
    AHEAD = 4
    ASIDES = (1, 1, 0, 1, 1, 2, 1, 2, 1, 1, 1, 2, 0, 4)
    ROUTE_STEPS = 18
    ROUTE_AT = (6, 0)
    WT_AT = (13, 12)

    with ExitStack() as ctx:
        def sb(name, shape, dt=F32):
            return ctx.enter_context(nc.sbuf_tensor(name, shape, dt))

        def sem(name):
            return ctx.enter_context(nc.semaphore(name))

        def full(t):
            return t.bitcast(F32)

        early_sb = sb("early_sb", [P, early.shape[1]])
        late_sb = sb("late_sb", [P, late.shape[1]])
        c_t = early_sb[:, 0:B]
        wmod = early_sb[:, B:B + 6 * D].rearrange("p (m n) -> p m n", m=6)
        o = 0
        wq = late_sb[:, o:o + D]; o += D
        wk = late_sb[:, o:o + D]; o += D
        wv = late_sb[:, o:o + D]; o += D
        router_w = late_sb[:, o:o + E]; o += E
        b1 = late_sb[:, o:o + NK].rearrange("p (e c) -> p e c", c=HC); o += NK
        sb2 = late_sb[:, o:o + 1]
        rb_sb = sb("rb_sb", [P, E])
        rb2_sb = sb("rb2_sb", [KW, D])
        rb2_hi = sb("rb2_hi", [KW, D], F32R)
        rb2_st = sb("rb2_st", [KW, D], F32R)
        ident = sb("ident", [P, P])
        order = sb("order", [P, E])
        half = sb("half", [P, T])
        euler = sb("euler", [P, T, E])
        w1_sb = sb("w1_sb", [P, NE, HC * P])
        w1_hi = sb("w1_hi", [P, NE, HC * P], F32R)
        w1_lo = sb("w1_lo", [P, NE, HC * P], F32R)
        w2_sb = sb("w2_sb", [P, NE, HC * D])
        w2_hi = sb("w2_hi", [P, NE, HC * D], F32R)
        w2_lo = sb("w2_lo", [P, NE, HC * D], F32R)
        silu_e = sb("silu_e", [P, B])
        silu_d = sb("silu_d", [P, B])
        silu_r = sb("silu_r", [P, B])
        silu_s = sb("silu_s", [P, B])
        SA, CA, SB, CB, GA, GB = range(6)
        IN_WMOD = (0, 1, 3, 4, 2, 5)
        cols = sb("cols", [P, 6, B])
        ca1 = sb("ca1", [P, B])
        cb1 = sb("cb1", [P, B])
        g_sign = sb("g_sign", [P, 2, B])
        g_unit = sb("g_unit", [P, 2, B])
        g_abs = sb("g_abs", [P, 2, B])
        g_cols = sb("g_cols", [P, 2, B])
        ga, gb = g_cols[:, 0], g_cols[:, 1]
        gbb2 = sb("gbb2", [P, B])
        sa_c = sb("sa_c", [P, B, P])
        wv_ga = sb("wv_ga", [P, B, D])
        wvt_ga = sb("wvt_ga", [P, B, D])
        vrow = sa_c
        wvg = wv_ga
        wvg_hi = sb("wvg_hi", [P, B, D], F32R)
        wvg_lo = sb("wvg_lo", [P, B, D], F32R)
        g_f = sb("g_f", [P, D])
        g_hi = sb("g_hi", [P, D], F32R)
        g_lo = sb("g_lo", [P, D], F32R)
        x_sb = sb("x_sb", [P, B, T, D])
        x1_sb = sb("x1_sb", [P, B, T, D])
        stats = sb("stats", [P, 2, B, T, 6])
        mv = sb("mv", [P, 2, B, T, 2])
        ve = sb("ve", [P, 2, B, T])
        rstd = sb("rstd", [P, 2, B, T])
        nh_sb = sb("nh_sb", [P, 4, T, D])
        n_sb = nh_sb[:, 0:2]
        ht = nh_sb[:, 2].rearrange("p t d -> p (t d)")
        n_hi = sb("n_hi", [P, 2, T, D], F32R)
        n_lo = sb("n_lo", [P, 2, T, D], F32R)
        ht_hi = sb("ht_hi", [P, 2, S], F32R)
        ht_lo = sb("ht_lo", [P, 2, S], F32R)
        q_hi = sb("q_hi", [P, 2, S], F32R)
        q_lo = sb("q_lo", [P, 2, S], F32R)
        nmax = sb("nmax", [P, B, T])
        rsum = sb("rsum", [P, B, T])
        rinv = sb("rinv", [P, B, T])
        n_mid = sb("n_mid", [P, T, D])
        p_sb = sb("p_sb", [P, T, S])
        pt_hi = sb("pt_hi", [P, HB, T, HT * P], F32R)
        pt_lo = sb("pt_lo", [P, HB, T, HT * P], F32R)
        ct_hi = sb("ct_hi", [P, HT * P], F32R)
        ct_lo = sb("ct_lo", [P, HT * P], F32R)
        n2_sb = sb("n2_sb", [P, T, D])
        lg = sb("lg", [P, B, T, E])
        lmax = sb("lmax", [P, B, T])
        le = sb("le", [P, B, T, E])
        ex = sb("ex", [P, B, T, E])
        es = sb("es", [P, T])
        er = sb("er", [P, T])
        pr = sb("pr", [P, T, E])
        pr_left = sb("pr_left", [P, T, E])
        top = sb("top", [P, T])
        is_top = sb("is_top", [P, T, E])
        first_of = sb("first_of", [P, T])
        chosen = sb("chosen", [P, 2, T, E])
        wt = sb("wt", [P, T, E])
        wst = sb("wst", [P, T, WHOLE + E])
        wt_t = sb("wt_t", [KW, 2, S], F32R)
        wt_rows = sb("wt_rows", [WHOLE + E, 2, S])
        wb = sb("wb", [P, E, S])
        h2 = sb("h2", [P, 2, S])
        h2_hi = sb("h2_hi", [P, B, S], F32R)
        h2_lo = sb("h2_lo", [P, B, S], F32R)
        SL = 4
        act_sb = p_sb
        t_sb = nh_sb[:].rearrange("p a t d -> p a (t d)")
        t_hi = pt_hi[:].rearrange("p a k q -> p (a k q)").rearrange("p (a s) -> p a s", a=SL)
        t_lo = pt_lo[:].rearrange("p a k q -> p (a k q)").rearrange("p (a s) -> p a s", a=SL)
        out_sb = x_sb[:, 0:2]
        y_sb = x_sb[:, 2:4].rearrange("p b t d -> p b (t d)")

        bank = [ctx.enter_context(nc.psum_tensor(f"bank{i}", [P, 512], F32)) for i in range(8)]
        s_ps, t_ps = bank[0:2], bank[2:4]
        a_ps, q_ps, c_ps, o_ps = bank[4:8]
        hid_ps = bank[0:AHEAD]
        acc_ps = bank[6:8]
        y_last_ps = (a_ps, q_ps)

        early_in = sem("early_in")
        x_in = [sem(f"x_in{b}") for b in range(B)]
        late_in = sem("late_in")
        small_in = sem("small_in")
        w1_in = sem("w1_in")
        w2_in = sem("w2_in")
        stored = [sem(f"stored{i}") for i in range(2)]
        stored_last = sem("stored_last")
        consts_ready = sem("consts_ready")
        silu_exp_ready = sem("silu_exp_ready")
        silu_steps = sem("silu_steps")
        modulation_mm = sem("modulation_mm")
        cols_ready = sem("cols_ready")
        cols1_ready = sem("cols1_ready")
        g_cols_steps = sem("g_cols_steps")
        wv_ga_ready = sem("wv_ga_ready")
        wv_ga_transposed = sem("wv_ga_transposed")
        wvt_ga_ready = sem("wvt_ga_ready")
        wvg_ready = sem("wvg_ready")
        vrow_mm = sem("vrow_mm")
        vrow_ready = sem("vrow_ready")
        sa_c_ready = sem("sa_c_ready")
        g_ready = sem("g_ready")
        g_split_steps = sem("g_split_steps")
        wvg_hi_ready = sem("wvg_hi_ready")
        wvg_lo_ready = sem("wvg_lo_ready")
        w_hi_ready = sem("w_hi_ready")
        w_lo_ready = sem("w_lo_ready")
        rb2_steps = sem("rb2_steps")
        stats1_ready = sem("stats1_ready")
        mean_var1_ready = sem("mean_var1_ready")
        var_eps1_ready = sem("var_eps1_ready")
        rstd1_ready = sem("rstd1_ready")
        centred = sem("centred")
        n_ready = sem("n_ready")
        vrow_added = sem("vrow_added")
        n_hi_ready = sem("n_hi_ready")
        n_lo_ready = sem("n_lo_ready")
        n_transposed = sem("n_transposed")
        ht_ready = sem("ht_ready")
        ht_hi_ready = sem("ht_hi_ready")
        ht_lo_ready = sem("ht_lo_ready")
        q_ready = sem("q_ready")
        q_hi_ready = sem("q_hi_ready")
        q_lo_ready = sem("q_lo_ready")
        scores_ready = sem("scores_ready")
        row_max_ready = sem("row_max_ready")
        probs_ready = sem("probs_ready")
        p_transposed = sem("p_transposed")
        pt_hi_ready = sem("pt_hi_ready")
        pt_lo_ready = sem("pt_lo_ready")
        context_ready = sem("context_ready")
        ct_hi_ready = sem("ct_hi_ready")
        ct_lo_ready = sem("ct_lo_ready")
        attention_ready = sem("attention_ready")
        rinv_ready = sem("rinv_ready")
        x1_ready = sem("x1_ready")
        stats2_ready = sem("stats2_ready")
        mean_var2_ready = sem("mean_var2_ready")
        var_eps2_ready = sem("var_eps2_ready")
        rstd2_ready = sem("rstd2_ready")
        n2_ready = sem("n2_ready")
        n2_transposed = sem("n2_transposed")
        h2_ready = sem("h2_ready")
        h2_hi_ready = sem("h2_hi_ready")
        h2_lo_ready = sem("h2_lo_ready")
        router_mm = sem("router_mm")
        logits_ready = sem("logits_ready")
        route_steps_done = sem("route_steps_done")
        router_exp_ready = sem("router_exp_ready")
        logit_max_ready = sem("logit_max_ready")
        logits_less_max_ready = sem("logits_less_max_ready")
        wst_ready = sem("wst_ready")
        wst_transposed = sem("wst_transposed")
        wt_rows_ready = sem("wt_rows_ready")
        wt_t_ready = sem("wt_t_ready")
        hidden_ready = sem("hidden_ready")
        gelu_ready = sem("gelu_ready")
        wb_in = {e: sem(f"wb_in{e}") for e in range(1, NE)}
        weighed_ready = sem("weighed_ready")
        t_hi_ready = sem("t_hi_ready")
        t_lo_ready = sem("t_lo_ready")
        accumulated = sem("accumulated")
        y_ready = sem("y_ready")
        y_transposed = sem("y_transposed")
        out_ready = sem("out_ready")

        block = ctx.enter_context(nc.Block())

        def q_pieces(b):
            return ((q_ps[:, 0:P], slice(0, P)), (c_ps[:, P:S], slice(P, S))) if b == 0 else ((q_ps[:], slice(0, S)),)

        def q_count(b, n):
            return b + 1 + (n if b == 0 else 1)

        def weighed(K):
            b, k = divmod(K, NK)
            return b * (NK - HC) + max(0, k + 1 - HC)

        @block.sync
        def _(sp):
            def load_x(b):
                sp.dma_start(x_sb[:, b], x[b].rearrange("(p t) d -> p t d", t=T)).then_inc(x_in[b], 16)

            load_x(0)
            sp.dma_start(early_sb[:], early).then_inc(early_in, 16)
            sp.dma_start(late_sb[:], late).then_inc(late_in, 16)
            for b in range(1, B):
                load_x(b)
            sp.dma_start(w1_sb[:], w1).then_inc(w1_in, 16)
            sp.dma_start(w2_sb[:], w2).then_inc(w2_in, 16)
            sp.wait_ge(consts_ready, 6)
            for q in (0, 32, 64):
                sp.dma_start(rb2_sb[q:q + E, :], rb2).then_inc(small_in, 16)
            sp.dma_start(rb_sb[:], router_b.to_broadcast([P, E])).then_inc(small_in, 16)

            def spread_weights(b):
                sp.wait_ge(wt_rows_ready, b + 1)
                for e in range(1, NE):
                    if b:
                        sp.wait_ge(weighed_ready, b * (NK - HC) - (NE - 1 - e) * HC)
                    row = wt_rows[WHOLE + e - 1:WHOLE + e, b % 2]
                    sp.dma_start(wb[:, e - 1], row[:, None].to_broadcast([1, P, S])).then_inc(wb_in[e], 16)

            def store(b):
                sp.wait_ge(out_ready, b + 1)
                sp.dma_start(out[b].rearrange("(p t) d -> p t d", t=T), out_sb[:, b % 2]).then_inc(stored[b % 2], 16)

            def store_half(h):
                ts = slice(h * HT, (h + 1) * HT)
                sp.wait_ge(out_ready, B + h)
                sp.dma_start(out[B - 1].rearrange("(p t) d -> p t d", t=T)[:, ts], out_sb[:, (B - 1) % 2, ts]).then_inc(stored_last, 16)

            for b in range(B):
                spread_weights(b)
                if b:
                    store(b - 1)
            for h in range(HB):
                store_half(h)
            for i in range(2):
                sp.wait_ge(stored[i], 16 * ((B - i) // 2))
            sp.wait_ge(stored_last, 16 * HB)

        @block.gpsimd
        def _(pool):
            pool.memset(half[:], -0.5).then_inc(consts_ready, 1)
            pool.memset(ident[:], 0.0).then_inc(consts_ready, 1)
            for e in range(E):
                i = pool.memset(order[:, e:e + 1], float(E - e))
            i.then_inc(consts_ready, 1)
            pool.memset(wst[:], 0.0).then_inc(consts_ready, 1)
            pool.memset(rb2_sb[:], 0.0).then_inc(consts_ready, 1)
            pool.memset(euler[:], math.e).then_inc(consts_ready, 1)
            pool.wait_ge(consts_ready, 6)
            pool.affine_select(out=ident[:], in_=ident[:], compare_op=ALU.not_equal, fill=1.0, base=0,
                               pattern=[[-1, P]], channel_multiplier=1).then_inc(consts_ready, 1)

            def rsqrt_var(n, b, ves, rss):
                pool.wait_ge(ves, b + 1)
                pool.tensor_tensor(rstd[:, n, b], ve[:, n, b], half[:], ALU.pow).then_inc(rss, 1)
                pool.wait_ge(rss, b + 1)

            def norm1(b):
                rsqrt_var(0, b, var_eps1_ready, rstd1_ready)
                if b < 2:
                    return
                normalise(0, b, x_sb, (n_transposed, n_hi_ready, n_lo_ready), b - 1, n_sb[:, b % 2], n_ready)

            def normalise(n, b, src, readers, read, dst, done):
                pool.tensor_tensor(n_mid[:], src[:, b], mv[:, n, b, :, 0:1].to_broadcast([P, T, D]), ALU.subtract).then_inc(centred, 1)
                pool.wait_ge(centred, b - 1 if n == 0 else b + B - 1)
                for reader in readers:
                    pool.wait_ge(reader, read)
                pool.tensor_tensor(dst, n_mid[:], rstd[:, n, b, :, None].to_broadcast([P, T, D]), ALU.mult).then_inc(done, 1)

            def norm2(b):
                rsqrt_var(1, b, var_eps2_ready, rstd2_ready)
                normalise(1, b, x1_sb, (n2_transposed,), b, n2_sb[:], n2_ready)

            def n_split_lo(b):
                pool.wait_ge(n_hi_ready, b + 1)
                pool.wait_ge(n_ready, b + 1)
                if b >= 2:
                    pool.wait_ge(context_ready, HB * (b - 1))
                pool.tensor_tensor(n_lo[:, b % 2], n_sb[:, b % 2], full(n_hi[:, b % 2]), ALU.subtract).then_inc(n_lo_ready, 1)

            def add_vrow(b):
                pool.wait_ge(vrow_ready, 1)
                pool.wait_ge(n_ready, b + 1)
                pool.tensor_tensor(x_sb[:, b], x_sb[:, b], vrow[:, b:b + 1].to_broadcast([P, T, D]), ALU.add).then_inc(vrow_added, 1)

            def router_exp(b):
                pool.wait_ge(logits_less_max_ready, b + 1)
                pool.tensor_tensor(ex[:, b], euler[:], le[:, b], ALU.pow).then_inc(router_exp_ready, 1)

            def h2_split_lo(b):
                pool.wait_ge(h2_hi_ready, b + 1)
                pool.tensor_tensor(h2_lo[:, b], h2[:, b % 2], full(h2_hi[:, b]), ALU.subtract).then_inc(h2_lo_ready, 1)

            def weights_lo(e):
                pool.wait_ge(w_hi_ready, e + 1)
                pool.tensor_tensor(w1_lo[:, e], w1_sb[:, e], full(w1_hi[:, e]), ALU.subtract)
                pool.tensor_tensor(w2_lo[:, e], w2_sb[:, e], full(w2_hi[:, e]), ALU.subtract).then_inc(w_lo_ready, 1)

            norm1(0)
            norm1(1)
            n_split_lo(0)
            pool.wait_ge(late_in, 16)
            pool.wait_ge(g_cols_steps, 4)
            pool.tensor_tensor(wv_ga[:], wv[:, None].to_broadcast([P, B, D]), ga[:, :, None].to_broadcast([P, B, D]),
                               ALU.mult).then_inc(wv_ga_ready, 1)
            for u in range(U):
                b, first = u // HB, u % HB == 0
                if first and b:
                    add_vrow(b - 1)
                    if u == 2:
                        pool.wait_ge(wvg_hi_ready, 1)
                        pool.tensor_tensor(wvg_lo[:], wvg[:], full(wvg_hi[:]), ALU.subtract).then_inc(wvg_lo_ready, 1)
                    n_split_lo(b)
                if u == U - 1:
                    h2_split_lo(0)
                if not first and b + 2 < B:
                    norm1(b + 2)
                if u == 1:
                    pool.wait_ge(wvt_ga_ready, 1)
                    pool.wait_ge(cols1_ready, 1)
                    pool.tensor_tensor(wvg[:], wvt_ga[:], ca1[:, :, None].to_broadcast([P, B, D]), ALU.mult).then_inc(wvg_ready, 1)
                if not first and b >= 2:
                    norm2(b - 2)
                if u >= 3:
                    for e in range(NE * (u - 3) // (U - 3), NE * (u - 2) // (U - 3)):
                        weights_lo(e)
            add_vrow(B - 1)
            norm2(B - 2)
            router_exp(1)
            norm2(B - 1)
            h2_split_lo(1)
            for b in range(2, B):
                h2_split_lo(b)
                router_exp(b)

        @block.scalar
        def _(act):
            act.wait_ge(early_in, 16)
            act.activation(silu_e[:], c_t, ACT.Exp, scale=-1.0).then_inc(silu_exp_ready, 1)

            def n_split_hi(b):
                act.wait_ge(n_ready, b + 1)
                if b >= 2:
                    act.wait_ge(context_ready, HB * (b - 1))
                    act.wait_ge(n_lo_ready, b - 1)
                act.activation(n_hi[:, b % 2], n_sb[:, b % 2], ACT.Copy).then_inc(n_hi_ready, 1)

            def ht_make(b):
                act.wait_ge(n_transposed, b + 1)
                if b == 0:
                    act.wait_ge(cols1_ready, 1)
                else:
                    act.wait_ge(ht_lo_ready, b)
                    act.wait_ge(ht_hi_ready, b)
                act.activation(ht, a_ps[:], ACT.Identity, scale=ca1[:, b:b + 1], bias=cols[:, SA, b:b + 1]).then_inc(ht_ready, 1)
                act.wait_ge(ht_ready, b + 1)
                if b >= 2:
                    act.wait_ge(scores_ready, T * (b - 1))
                    act.wait_ge(ht_lo_ready, b - 1)
                act.activation(ht_hi[:, b % 2], ht, ACT.Copy).then_inc(ht_hi_ready, 1)

            def q_split_hi(b):
                if b >= 2:
                    act.wait_ge(scores_ready, T * (b - 1))
                    act.wait_ge(q_lo_ready, b)
                for n, (ps, cs) in enumerate(q_pieces(b)):
                    act.wait_ge(q_ready, q_count(b, n))
                    act.activation(q_hi[:, b % 2, cs], ps, ACT.Copy).then_inc(q_hi_ready, 1)

            def exps(n):
                b, t = divmod(n, T)
                act.wait_ge(row_max_ready, n + 1)
                if b:
                    act.wait_ge(p_transposed, n - T + 1)
                act.activation(p_sb[:, t], s_ps[n % 2][:], ACT.Exp, bias=nmax[:, b, t:t + 1],
                               accum_out=rsum[:, b, t:t + 1]).then_inc(probs_ready, 1)

            def pt_split_hi(n):
                u, i = divmod(n, HT)
                act.wait_ge(p_transposed, n + 1)
                if u >= 2:
                    act.wait_ge(context_ready, u - 1)
                    act.wait_ge(pt_lo_ready, HT * (u - 1))
                act.activation(pt_hi[:, u % 2, :, i * P:(i + 1) * P], t_ps[n % 2][:].rearrange("p (k q) -> p k q", k=T),
                               ACT.Copy).then_inc(pt_hi_ready, 1)

            def c_split_hi(u):
                act.wait_ge(context_ready, u + 1)
                if u:
                    act.wait_ge(attention_ready, u)
                    act.wait_ge(ct_lo_ready, u)
                act.activation(ct_hi[:], c_ps[:, 0:HT * P], ACT.Copy).then_inc(ct_hi_ready, 1)

            def h2_make(b):
                act.wait_ge(n2_transposed, b + 1)
                act.wait_ge(cols1_ready, 2)
                if b >= 2:
                    act.wait_ge(h2_lo_ready, b - 1)
                    act.wait_ge(router_mm, b - 1)
                act.activation(h2[:, b % 2], a_ps[:], ACT.Identity, scale=cb1[:, b:b + 1], bias=cols[:, SB, b:b + 1]).then_inc(h2_ready, 1)
                act.wait_ge(h2_ready, b + 1)
                act.activation(h2_hi[:, b], h2[:, b % 2], ACT.Copy).then_inc(h2_hi_ready, 1)

            def weights_hi(e):
                if e == 0:
                    act.wait_ge(w1_in, 16)
                    act.wait_ge(w2_in, 16)
                act.activation(w1_hi[:, e], w1_sb[:, e], ACT.Copy)
                act.activation(w2_hi[:, e], w2_sb[:, e], ACT.Copy).then_inc(w_hi_ready, 1)

            def router_exp(b):
                act.wait_ge(logits_less_max_ready, b + 1)
                act.activation(ex[:, b], le[:, b], ACT.Exp).then_inc(router_exp_ready, 1)

            ht_make(0)
            n_split_hi(0)
            q_split_hi(0)
            ht_make(1)
            for u in range(U + 1):
                b, first = u // HB, u % HB == 0
                for i in range(HT):
                    if i == 0 and first and 0 < b < B - 1:
                        ht_make(b + 1)
                    if u:
                        pt_split_hi(HT * (u - 1) + i)
                    if i == 0 and not first and b + 1 < B:
                        q_split_hi(b + 1)
                    if u < U:
                        exps(HT * u + i)
                    if i == 0 and first and 0 < b < B:
                        n_split_hi(b)
                    if i == 0 and u == U - 2:
                        h2_make(0)
                    if i == 0 and u == U - 1:
                        router_exp(0)
                if u >= 2:
                    c_split_hi(u - 2)
                if u == 0:
                    act.wait_ge(wv_ga_transposed, 1)
                    act.activation(wvt_ga[:], o_ps[:].rearrange("p (b d) -> p b d", b=B), ACT.Copy).then_inc(wvt_ga_ready, 1)
                if u == 1:
                    act.wait_ge(vrow_mm, 1)
                    act.activation(vrow[:], c_ps[:].rearrange("p (b d) -> p b d", b=B), ACT.Copy).then_inc(vrow_ready, 1)
                if u == 1:
                    act.wait_ge(wvg_ready, 1)
                    act.activation(wvg_hi[:], wvg[:], ACT.Copy).then_inc(wvg_hi_ready, 1)
                if 2 <= u < U:
                    for e in range(NE * (u - 2) // (U - 2), NE * (u - 1) // (U - 2)):
                        weights_hi(e)

            def gelus(K):
                b, k = divmod(K, NK)
                act.wait_ge(hidden_ready, K + 1)
                if K >= SL:
                    if (K - SL) % NK < HC:
                        act.wait_ge(t_hi_ready, K - SL + 1)
                        act.wait_ge(t_lo_ready, K - SL + 1)
                    else:
                        act.wait_ge(weighed_ready, weighed(K - SL))
                act.activation(act_sb[:, K % SL], hid_ps[K % AHEAD][:], ACT.Gelu, bias=b1[:, k // HC, k % HC:k % HC + 1]).then_inc(gelu_ready, 1)

            def split_hi(K):
                k = K % NK
                if k < HC:
                    act.wait_ge(gelu_ready, K + 1)
                else:
                    act.wait_ge(weighed_ready, weighed(K))
                if K % 2 == 0 and K < SL:
                    act.wait_ge(context_ready, U - 1 + K // 2)
                if K >= SL:
                    act.wait_ge(accumulated, K - SL + 1)
                    act.wait_ge(t_lo_ready, K - SL + 1)
                src = act_sb if k < HC else t_sb
                act.activation(t_hi[:, K % SL], src[:, K % SL], ACT.Copy).then_inc(t_hi_ready, 1)

            def weight_rows(b):
                act.wait_ge(wst_transposed, b + 1)
                if b >= 2:
                    for e in range(1, NE):
                        act.wait_ge(wb_in[e], 16 * (b - 1))
                act.activation(wt_rows[WHOLE:, b % 2], a_ps[WHOLE:WHOLE + E, :], ACT.Copy).then_inc(wt_rows_ready, 1)

            def y_evac(b, cs=slice(0, S)):
                act.wait_ge(accumulated, (b + 1) * NK)
                if b >= 2:
                    act.wait_ge(y_transposed, b - 1)
                act.activation(y_sb[:, b % 2, cs], acc_ps[b % 2][:, cs], ACT.Identity, scale=gb[:, b:b + 1],
                               bias=gbb2[:, b:b + 1]).then_inc(y_ready, 1)

            gelus(0)
            h2_make(1)
            gelus(1)
            c_split_hi(U - 1)
            for K in range(B * NK):
                b, k = divmod(K, NK)
                if 2 <= K + 1 < B * NK:
                    gelus(K + 1)
                for late, when in H2_LATE:
                    if K == when + 2:
                        h2_make(late)
                split_hi(K)
                if K == 0:
                    weight_rows(0)
                if b + 1 < B and k == WT_AT[b > 0] + 2:
                    weight_rows(b + 1)
                if b and k == 2:
                    y_evac(b - 1)
            for h in range(HB):
                y_evac(B - 1, slice(h * HT * P, (h + 1) * HT * P))

        @block.vector
        def _(dve):
            def layer_stats(n, b, src, sts, t0, t1):
                for t in range(t0, t1):
                    i = dve.bn_stats(stats[:, n, b, t], src[:, b, t])
                i.then_inc(sts, 1)

            def layer_mean_var(n, b, sts, mvs, ves):
                dve.wait_ge(sts, (b + 1) * (1 if n == 0 else HB))
                for t in range(T):
                    i = dve.bn_aggr(mv[:, n, b, t], stats[:, n, b, t])
                i.then_inc(mvs, 1)
                dve.wait_ge(mvs, b + 1)
                dve.tensor_scalar(ve[:, n, b], mv[:, n, b, :, 1], EPS, None, ALU.add).then_inc(ves, 1)

            def stats1(b):
                dve.wait_ge(x_in[b], 16)
                layer_stats(0, b, x_sb, stats1_ready, 0, T)
                layer_mean_var(0, b, stats1_ready, mean_var1_ready, var_eps1_ready)

            def norm1(b, t0, t1):
                dve.wait_ge(rstd1_ready, b + 1)
                for t in range(t0, t1):
                    i = dve.tensor_scalar(n_sb[:, b, t], x_sb[:, b, t], mv[:, 0, b, t, 0:1], rstd[:, 0, b, t:t + 1],
                                          ALU.subtract, ALU.mult)
                if t1 == T:
                    i.then_inc(n_ready, 1)

            def ht_split_lo(b):
                dve.wait_ge(ht_hi_ready, b + 1)
                if b >= 2:
                    dve.wait_ge(scores_ready, T * (b - 1))
                dve.tensor_tensor(ht_lo[:, b % 2], ht, full(ht_hi[:, b % 2]), ALU.subtract).then_inc(ht_lo_ready, 1)

            def q_split_lo(b, n=0):
                ps, cs = q_pieces(b)[n]
                dve.wait_ge(q_hi_ready, q_count(b, n))
                if b >= 2:
                    dve.wait_ge(scores_ready, T * (b - 1))
                dve.tensor_tensor(q_lo[:, b % 2, cs], ps, full(q_hi[:, b % 2, cs]), ALU.subtract).then_inc(q_lo_ready, 1)

            def row_max(n):
                dve.wait_ge(scores_ready, n + 1)
                dve.tensor_reduce(nmax[:, n // T, n % T:n % T + 1], s_ps[n % 2][:], AX.X, ALU.max, negate=True).then_inc(row_max_ready, 1)

            def pt_split_lo(n):
                u, i = divmod(n, HT)
                dve.wait_ge(pt_hi_ready, n + 1)
                if u >= 2:
                    dve.wait_ge(context_ready, u - 1)
                dve.tensor_tensor(pt_lo[:, u % 2, :, i * P:(i + 1) * P], t_ps[n % 2][:].rearrange("p (k q) -> p k q", k=T),
                                  full(pt_hi[:, u % 2, :, i * P:(i + 1) * P]), ALU.subtract).then_inc(pt_lo_ready, 1)

            def c_split_lo(u):
                dve.wait_ge(ct_hi_ready, u + 1)
                if u:
                    dve.wait_ge(attention_ready, u)
                dve.tensor_tensor(ct_lo[:], c_ps[:, 0:HT * P], full(ct_hi[:]), ALU.subtract).then_inc(ct_lo_ready, 1)

            def row_sums(u):
                b, t0 = u // HB, HT * (u % HB)
                dve.wait_ge(probs_ready, HT * (u + 1))
                dve.reciprocal(rinv[:, b, t0:t0 + HT], rsum[:, b, t0:t0 + HT]).then_inc(rinv_ready, 1)

            def residual(u):
                b, t0 = u // HB, HT * (u % HB)
                dve.wait_ge(rinv_ready, u + 1)
                dve.wait_ge(attention_ready, u + 1)
                dve.wait_ge(vrow_added, b + 1)
                for t in range(t0, t0 + HT):
                    i = dve.scalar_tensor_tensor(x1_sb[:, b, t], o_ps[:, (t - t0) * D:(t - t0 + 1) * D], rinv[:, b, t:t + 1],
                                                 x_sb[:, b, t], ALU.mult, ALU.add)
                i.then_inc(x1_ready, 1)

            def stats2(u):
                b, t0 = u // HB, HT * (u % HB)
                dve.wait_ge(x1_ready, u + 1)
                layer_stats(1, b, x1_sb, stats2_ready, t0, t0 + HT)
                if u % HB == HB - 1:
                    layer_mean_var(1, b, stats2_ready, mean_var2_ready, var_eps2_ready)

            def router_logits(b):
                dve.wait_ge(router_mm, b + 1)
                if b == 0:
                    dve.wait_ge(small_in, 64)
                dve.tensor_tensor(lg[:, b], (o_ps if b else q_ps)[:, 0:T * E].rearrange("p (t e) -> p t e", t=T),
                                  rb_sb[:, None, :].to_broadcast([P, T, E]), ALU.add).then_inc(logits_ready, 1)
                dve.wait_ge(logits_ready, b + 1)
                dve.tensor_reduce(lmax[:, b], lg[:, b], AX.X, ALU.max).then_inc(logit_max_ready, 1)
                dve.wait_ge(logit_max_ready, b + 1)
                dve.tensor_tensor(le[:, b], lg[:, b], lmax[:, b, :, None].to_broadcast([P, T, E]), ALU.subtract).then_inc(logits_less_max_ready, 1)

            def router_steps(b):
                count = [ROUTE_STEPS * b]

                def step(make, *args):
                    if count[0]:
                        dve.wait_ge(route_steps_done, count[0])
                    make(*args).then_inc(route_steps_done, 1)
                    count[0] += 1

                def by_token(a):
                    return a[:, :, None].to_broadcast([P, T, E])

                dve.wait_ge(router_exp_ready, b + 1)
                step(dve.tensor_reduce, es[:], ex[:, b], AX.X, ALU.add)
                yield
                step(dve.reciprocal, er[:], es[:])
                yield
                step(dve.tensor_tensor, pr[:], ex[:, b], by_token(er), ALU.mult)
                yield
                for n, left in enumerate((pr, pr_left)):
                    step(dve.tensor_reduce, top[:], left[:], AX.X, ALU.max)
                    yield
                    step(dve.tensor_tensor, is_top[:], left[:], by_token(top), ALU.is_ge)
                    yield
                    step(dve.tensor_tensor, is_top[:], is_top[:], order[:, None].to_broadcast([P, T, E]), ALU.mult)
                    yield
                    step(dve.tensor_reduce, first_of[:], is_top[:], AX.X, ALU.max)
                    yield
                    step(dve.tensor_tensor, chosen[:, n], is_top[:], by_token(first_of), ALU.is_equal)
                    yield
                    if n == 0:
                        step(dve.scalar_tensor_tensor, pr_left[:], chosen[:, 0], -2.0, pr[:], ALU.mult, ALU.add)
                        yield
                step(dve.tensor_tensor, chosen[:, 0], chosen[:, 0], chosen[:, 1], ALU.add)
                yield
                step(dve.tensor_tensor, wt[:], chosen[:, 0], pr[:], ALU.mult)
                yield
                if b:
                    dve.wait_ge(wst_transposed, b)
                step(dve.tensor_copy, wst[:, :, 0:E].bitcast(F32R), wt[:])
                yield
                dve.tensor_copy(wst[:, :, 64:64 + E].bitcast(F32R), wt[:])
                step(dve.tensor_copy, wst[:, :, WHOLE:WHOLE + E], wt[:])
                assert count[0] == ROUTE_STEPS * (b + 1)
                dve.tensor_tensor(wst[:, :, 32:32 + E].bitcast(F32R), wt[:], wst[:, :, 0:E], ALU.subtract).then_inc(wst_ready, 1)
                yield

            def weights_t(b):
                dve.wait_ge(wt_rows_ready, b + 1)
                if b >= 2:
                    dve.wait_ge(accumulated, (b - 1) * NK)
                dve.tensor_copy(wt_t[:, b % 2], a_ps[0:KW, :]).then_inc(wt_t_ready, 1)

            stats1(0)
            dve.wait_ge(silu_exp_ready, 1)
            dve.tensor_scalar(silu_d[:], silu_e[:], 1.0, None, ALU.add).then_inc(silu_steps, 1)
            dve.wait_ge(silu_steps, 1)
            dve.reciprocal(silu_r[:], silu_d[:]).then_inc(silu_steps, 1)
            dve.wait_ge(silu_steps, 2)
            dve.tensor_tensor(silu_s[:], silu_r[:], c_t, ALU.mult).then_inc(silu_steps, 1)
            norm1(0, 0, T)
            dve.wait_ge(modulation_mm, 1)
            dve.tensor_copy(cols[:, SA:CA + 1], t_ps[0][:, 0:2 * B].rearrange("p (m b) -> p m b", m=2)).then_inc(cols_ready, 1)
            dve.wait_ge(cols_ready, 1)
            dve.tensor_scalar(ca1[:], cols[:, CA], 1.0, None, ALU.add).then_inc(cols1_ready, 1)
            stats1(1)
            dve.wait_ge(g_ready, 1)
            dve.tensor_scalar(g_f[:], q_ps[:, 0:D], SCALE, None, ALU.mult).then_inc(g_split_steps, 1)
            dve.wait_ge(g_split_steps, 1)
            dve.tensor_copy(g_hi[:], g_f[:]).then_inc(g_split_steps, 1)
            dve.wait_ge(g_split_steps, 2)
            dve.tensor_tensor(g_lo[:], g_f[:], full(g_hi[:]), ALU.subtract).then_inc(g_split_steps, 1)
            ht_split_lo(0)
            dve.wait_ge(modulation_mm, 2)
            dve.tensor_copy(cols[:, SB:GB + 1], t_ps[1][:, 0:4 * B].rearrange("p (m b) -> p m b", m=4)).then_inc(cols_ready, 1)
            norm1(1, 0, 1)
            dve.wait_ge(cols_ready, 2)
            dve.tensor_scalar(g_sign[:], cols[:, GA:GB + 1], 0.0, 2.0, ALU.is_ge, ALU.mult).then_inc(g_cols_steps, 1)
            dve.tensor_scalar(cb1[:], cols[:, CB], 1.0, None, ALU.add).then_inc(cols1_ready, 1)
            norm1(1, 1, 2)
            dve.wait_ge(g_cols_steps, 1)
            dve.tensor_scalar(g_unit[:], g_sign[:], -1.0, None, ALU.add).then_inc(g_cols_steps, 1)
            norm1(1, 2, 3)
            dve.wait_ge(g_cols_steps, 2)
            dve.tensor_tensor(g_abs[:], g_unit[:], cols[:, GA:GB + 1], ALU.mult).then_inc(g_cols_steps, 1)
            norm1(1, 3, T)
            dve.wait_ge(g_cols_steps, 3)
            dve.scalar_tensor_tensor(g_cols[:], g_abs[:], 0.25, g_unit[:], ALU.max, ALU.mult).then_inc(g_cols_steps, 1)
            q_split_lo(0, 0)
            dve.wait_ge(x_in[2], 16)
            layer_stats(0, 2, x_sb, stats1_ready, 0, T)
            q_split_lo(0, 1)
            dve.tensor_copy(sa_c[:], cols[:, SA, :, None].to_broadcast([P, B, P])).then_inc(sa_c_ready, 1)
            dve.wait_ge(g_cols_steps, 4)
            dve.tensor_scalar(gbb2[:], gb, sb2, None, ALU.mult).then_inc(g_cols_steps, 1)
            layer_mean_var(0, 2, stats1_ready, mean_var1_ready, var_eps1_ready)

            def set_up(u):
                if u == 0:
                    ht_split_lo(1)
                if u == 5:
                    dve.wait_ge(small_in, 64)
                    dve.tensor_copy(rb2_hi[:], rb2_sb[:]).then_inc(rb2_steps, 1)
                    dve.wait_ge(rb2_steps, 1)
                    dve.tensor_copy(rb2_st[0:64], full(rb2_hi[0:64]))
                    dve.tensor_tensor(rb2_st[64:KW], rb2_sb[64:KW], full(rb2_hi[64:KW]), ALU.subtract).then_inc(rb2_steps, 1)

            route = router_steps(0)
            asides = iter(ASIDES)

            def aside(u):
                if u >= U - 1:
                    for _ in range(next(asides)):
                        next(route)

            for u in range(U + 1):
                b, first = u // HB, u % HB == 0
                if u < U:
                    row_max(HT * u)
                    if u == U - 1:
                        router_logits(0)
                    if u >= 4:
                        stats2(u - 4)
                    if u >= 3:
                        row_sums(u - 3)
                    row_max(HT * u + 1)
                    aside(u)
                else:
                    stats2(u - 4)
                    row_sums(u - 3)
                if u:
                    if not first and b + 1 < B:
                        q_split_lo(b + 1)
                    pt_split_lo(HT * (u - 1))
                    aside(u)
                    if first and b < B - 1:
                        ht_split_lo(b + 1)
                    pt_split_lo(HT * (u - 1) + 1)
                    aside(u)
                if u >= 3:
                    residual(u - 3)
                    aside(u)
                if u >= 2:
                    c_split_lo(u - 2)
                    aside(u)
                if not first and b + 3 < B:
                    stats1(b + 3)
                if u < U:
                    set_up(u)
                aside(u)
            stats2(U - 3)
            row_sums(U - 2)
            aside(U)
            row_sums(U - 1)
            aside(U)
            residual(U - 2)
            aside(U)
            c_split_lo(U - 1)
            residual(U - 1)

            def weigh(K):
                b, k = divmod(K, NK)
                if k < HC:
                    return
                e = k // HC
                dve.wait_ge(gelu_ready, K + 1)
                dve.wait_ge(wb_in[e], 16 * (b + 1))
                if K >= SL:
                    dve.wait_ge(t_hi_ready, K - SL + 1)
                    dve.wait_ge(t_lo_ready, K - SL + 1)
                dve.tensor_tensor(t_sb[:, K % SL], act_sb[:, K % SL], wb[:, e - 1], ALU.mult).then_inc(weighed_ready, 1)

            def split_lo(K):
                k = K % NK
                dve.wait_ge(t_hi_ready, K + 1)
                if K >= SL:
                    dve.wait_ge(accumulated, K - SL + 1)
                src = act_sb if k < HC else t_sb
                dve.tensor_tensor(t_lo[:, K % SL], src[:, K % SL], full(t_hi[:, K % SL]), ALU.subtract).then_inc(t_lo_ready, 1)

            def output(b):
                dve.wait_ge(y_transposed, b + 1)
                if b >= 2:
                    dve.wait_ge(stored[b % 2], 16 * (b // 2))
                dve.tensor_tensor(out_sb[:, b % 2].rearrange("p t d -> p (t d)"), a_ps[:],
                                  x1_sb[:, b].rearrange("p t d -> p (t d)"), ALU.add).then_inc(out_ready, 1)

            def output_half(h):
                ts = slice(h * HT, (h + 1) * HT)
                dve.wait_ge(y_transposed, B + h)
                if h == 0 and B > 2:
                    dve.wait_ge(stored[(B - 1) % 2], 16 * ((B - 1) // 2))
                dve.tensor_tensor(out_sb[:, (B - 1) % 2, ts], y_last_ps[h][:, 0:HT * P].rearrange("p (t d) -> p t d", t=HT),
                                  x1_sb[:, B - 1, ts], ALU.add).then_inc(out_ready, 1)

            for K in range(B * NK):
                b, k = divmod(K, NK)
                if K == HC - 1:
                    split_lo(K)
                    stats2(U - 2)
                    stats2(U - 1)
                if K + 1 < B * NK:
                    weigh(K + 1)
                if b + 1 < B:
                    if k == ROUTE_AT[b > 0]:
                        route = router_steps(b + 1)
                    if k >= ROUTE_AT[b > 0]:
                        next(route, None)
                if K != HC - 1:
                    split_lo(K)
                if K == HC:
                    weights_t(0)
                for late, when in LOGITS_LATE:
                    if K == when + 1:
                        router_logits(late)
                if b + 1 < B:
                    if k >= ROUTE_AT[b > 0] and (b == 0 or k < 5):
                        next(route, None)
                    if b == 0 and k >= ROUTE_AT[0] + 3:
                        next(route, None)
                    if k == WT_AT[b > 0] + 3:
                        weights_t(b + 1)
                if b and k == 6:
                    output(b - 1)
            for h in range(HB):
                output_half(h)

        @block.tensor
        def _(pe):
            def product(ps, lhs, rhs, start=True, stop=True):
                pe.matmul(ps, lhs[0], rhs[0], start=start, stop=False)
                pe.matmul(ps, lhs[0], rhs[1], start=False, stop=False)
                return pe.matmul(ps, lhs[1], rhs[0], start=False, stop=stop)

            def n_transposes(b):
                pe.wait_ge(n_ready, b + 1)
                if b == 0:
                    pe.wait_ge(consts_ready, 7)
                else:
                    pe.wait_ge(ht_ready, b)
                for t in range(T):
                    i = pe.transpose(a_ps[:, t * P:(t + 1) * P], n_sb[:, b % 2, t], ident[:])
                i.then_inc(n_transposed, 1)

            def q_project(b):
                pe.wait_ge(ht_hi_ready, b + 1)
                pe.wait_ge(ht_lo_ready, b + 1)
                if b == 0:
                    pe.wait_ge(g_split_steps, 3)
                else:
                    pe.wait_ge(q_lo_ready, b + 1)
                for ps, cs in q_pieces(b):
                    i = product(ps, (g_hi[:], g_lo[:]), (ht_hi[:, b % 2, cs], ht_lo[:, b % 2, cs])).then_inc(q_ready, 1)

            def scores(n):
                b, t = divmod(n, T)
                if t == 0 or n == 1:
                    pe.wait_ge(q_hi_ready, b + 1 + (n > 0))
                    pe.wait_ge(q_lo_ready, b + 1 + (n > 0))
                if n >= 2:
                    pe.wait_ge(probs_ready, n - 1)
                cs = slice(t * P, (t + 1) * P)
                product(s_ps[n % 2][:], (q_hi[:, b % 2, cs], q_lo[:, b % 2, cs]), (ht_hi[:, b % 2], ht_lo[:, b % 2])).then_inc(scores_ready, 1)

            def p_transposes(n):
                pe.wait_ge(probs_ready, n + 1)
                if n >= 2:
                    pe.wait_ge(pt_lo_ready, n - 1)
                else:
                    pe.wait_ge(cols_ready, n + 1)
                for k in range(T):
                    i = pe.transpose(t_ps[n % 2][:, k * P:(k + 1) * P], p_sb[:, n % T, k * P:(k + 1) * P], ident[:])
                i.then_inc(p_transposed, 1)

            def context(u):
                b = u // HB
                pe.wait_ge(n_hi_ready, b + 1)
                pe.wait_ge(n_lo_ready, b + 1)
                pe.wait_ge(pt_lo_ready, HT * (u + 1))
                if u:
                    pe.wait_ge(ct_lo_ready, u)
                else:
                    pe.wait_ge(vrow_ready, 1)
                for k in range(T):
                    i = product(c_ps[:, 0:HT * P], (n_hi[:, b % 2, k], n_lo[:, b % 2, k]), (pt_hi[:, u % 2, k], pt_lo[:, u % 2, k]),
                                start=(k == 0), stop=(k == T - 1))
                i.then_inc(context_ready, 1)

            def project_out(u):
                b = u // HB
                pe.wait_ge(ct_lo_ready, u + 1)
                if u == 0:
                    pe.wait_ge(wvg_lo_ready, 1)
                else:
                    pe.wait_ge(x1_ready, u)
                for t in range(HT):
                    cs = slice(t * P, (t + 1) * P)
                    i = product(o_ps[:, t * D:(t + 1) * D], (ct_hi[:, cs], ct_lo[:, cs]), (wvg_hi[:, b], wvg_lo[:, b]))
                i.then_inc(attention_ready, 1)

            def n2_transposes(b):
                pe.wait_ge(n2_ready, b + 1)
                pe.wait_ge(ht_ready, B)
                if b:
                    pe.wait_ge(h2_ready, b)
                if b >= 2:
                    pe.wait_ge(wt_t_ready, 1)
                for t in range(T):
                    i = pe.transpose(a_ps[:, t * P:(t + 1) * P], n2_sb[:, t], ident[:])
                i.then_inc(n2_transposed, 1)

            def router(b):
                pe.wait_ge(h2_ready, b + 1)
                if b == 0:
                    pe.wait_ge(q_lo_ready, B + 1)
                if b:
                    pe.wait_ge(x1_ready, U)
                    pe.wait_ge(logits_ready, b)
                for t in range(T):
                    i = pe.matmul((o_ps if b else q_ps)[:, t * E:(t + 1) * E], h2[:, b % 2, t * P:(t + 1) * P], router_w, start=True, stop=True)
                i.then_inc(router_mm, 1)

            def w_transposes(b):
                pe.wait_ge(wst_ready, b + 1)
                pe.wait_ge(h2_ready, B - 2 if b == 0 else B)
                if b:
                    pe.wait_ge(wt_t_ready, b)
                if b >= 2:
                    pe.wait_ge(out_ready, b - 1)
                for t in range(T):
                    i = pe.transpose(a_ps[0:WHOLE + E, t * P:(t + 1) * P], wst[:, t], ident[:])
                i.then_inc(wst_transposed, 1)

            def modulation(ps, parts):
                for n, m in enumerate(parts):
                    i = pe.matmul(ps[:, n * B:(n + 1) * B], wmod[:, IN_WMOD[m]], silu_s[:], start=True, stop=True)
                i.then_inc(modulation_mm, 1)

            pe.wait_ge(silu_steps, 3)
            modulation(t_ps[0], (SA, CA))
            n_transposes(0)
            pe.wait_ge(late_in, 16)
            pe.matmul(q_ps[:, 0:D], wq, wk, start=True, stop=True).then_inc(g_ready, 1)
            modulation(t_ps[1], (SB, CB, GA, GB))
            q_project(0)
            n_transposes(1)
            for u in range(U + 1):
                b, first = u // HB, u % HB == 0
                for i in range(HT):
                    if i == 0 and first and 0 < b < B - 1:
                        n_transposes(b + 1)
                    if u < U:
                        scores(HT * u + i)
                    if u:
                        p_transposes(HT * (u - 1) + i)
                    if i == 0 and not first and b + 1 < B:
                        q_project(b + 1)
                    if i == 0 and u == U - 2:
                        n2_transposes(0)
                if u == 0:
                    pe.wait_ge(wv_ga_ready, 1)
                    for n in range(B):
                        i = pe.transpose(o_ps[:, n * D:(n + 1) * D], wv_ga[:, n], ident[:])
                    i.then_inc(wv_ga_transposed, 1)
                if u == 1:
                    pe.wait_ge(wvt_ga_ready, 1)
                    pe.wait_ge(sa_c_ready, 1)
                    for n in range(B):
                        i = pe.matmul(c_ps[:, n * D:(n + 1) * D], sa_c[:, n], wvt_ga[:, n], start=True, stop=True)
                    i.then_inc(vrow_mm, 1)
                if u >= 3:
                    project_out(u - 3)
                if u >= 2:
                    context(u - 2)
                if u == U - 2:
                    router(0)

            def hidden(K):
                b, k = divmod(K, NK)
                e, c = divmod(k, HC)
                if k == 0:
                    pe.wait_ge(h2_hi_ready, b + 1)
                    pe.wait_ge(h2_lo_ready, b + 1)
                if b == 0 and c == 0:
                    pe.wait_ge(w_lo_ready, e + 1)
                if K < 2:
                    pe.wait_ge(probs_ready, T * B - 1 + K)
                elif K < AHEAD:
                    pe.wait_ge(pt_lo_ready, T * B - 3 + K)
                else:
                    pe.wait_ge(gelu_ready, K - AHEAD + 1)
                cs = slice(c * P, (c + 1) * P)
                product(hid_ps[K % AHEAD][:], (w1_hi[:, e, cs], w1_lo[:, e, cs]), (h2_hi[:, b], h2_lo[:, b])).then_inc(hidden_ready, 1)

            def accumulate(K):
                b, k = divmod(K, NK)
                e, c = divmod(k, HC)
                if K == 0:
                    pe.wait_ge(ct_lo_ready, U)
                if k == 0 and b == 1:
                    pe.wait_ge(logits_ready, B)
                if k == 0 and b >= 2:
                    pe.wait_ge(y_ready, b - 1)
                pe.wait_ge(t_hi_ready, K + 1)
                pe.wait_ge(t_lo_ready, K + 1)
                cs = slice(c * D, (c + 1) * D)
                i = product(acc_ps[b % 2][:], (w2_hi[:, e, cs], w2_lo[:, e, cs]), (t_hi[:, K % SL], t_lo[:, K % SL]),
                            start=(k == 0), stop=(k == NK - 1))
                i.then_inc(accumulated, 1)

            def expert_bias(b):
                pe.wait_ge(wt_t_ready, b + 1)
                if b == 0:
                    pe.wait_ge(rb2_steps, 2)
                pe.matmul(acc_ps[b % 2][:], rb2_st[:], wt_t[:, b % 2], start=False, stop=False)

            def y_transposes(b):
                pe.wait_ge(y_ready, b + 1)
                pe.wait_ge(wt_t_ready, min(b + 2, B))
                if b:
                    pe.wait_ge(out_ready, b)
                for t in range(T):
                    i = pe.transpose(a_ps[:, t * P:(t + 1) * P], y_sb[:, b % 2, t * P:(t + 1) * P], ident[:])
                i.then_inc(y_transposed, 1)

            def y_transposes_half(h):
                pe.wait_ge(y_ready, B + h)
                pe.wait_ge(out_ready, B - 1)
                pe.wait_ge(logits_ready, B)
                for t in range(HT):
                    n = h * HT + t
                    i = pe.transpose(y_last_ps[h][:, t * P:(t + 1) * P], y_sb[:, (B - 1) % 2, n * P:(n + 1) * P], ident[:])
                i.then_inc(y_transposed, 1)

            hidden(0)
            n2_transposes(1)
            hidden(1)
            project_out(U - 2)
            context(U - 1)
            hidden(2)
            w_transposes(0)
            project_out(U - 1)
            hidden(3)
            for K in range(B * NK):
                b, k = divmod(K, NK)
                n = K + AHEAD
                if n < B * NK:
                    hidden(n)
                if b + 1 < B and k == WT_AT[b > 0]:
                    w_transposes(b + 1)
                for late, when in H2_LATE:
                    if K == when:
                        n2_transposes(late)
                for late, when in LOGITS_LATE:
                    if K == when:
                        router(late)
                accumulate(K)
                if k == 3:
                    expert_bias(b)
                if b and k == 4:
                    y_transposes(b - 1)
            for h in range(HB):
                y_transposes_half(h)


def kernel(L0_attn_x, L0_attn_Wq, L0_attn_Wk, L0_attn_Wv, L0_ffn_router_w, L0_ffn_router_b, L0_ffn_sw1, L0_ffn_sb1,
           L0_ffn_sw2, L0_ffn_sb2, L0_ffn_rw1, L0_ffn_rb1, L0_ffn_rw2, L0_ffn_rb2, L0_c, L0_wmod):
    import numpy as np
    import concourse.bacc as bacc
    from concourse.bass_utils import run_bass_kernel_spmd

    f = lambda a: np.asarray(a)
    E, D, H = f(L0_ffn_rw1).shape
    hc = H // P
    w1 = np.concatenate([f(L0_ffn_sw1)[None], f(L0_ffn_rw1)]).transpose(1, 0, 2)
    w2 = np.concatenate([f(L0_ffn_sw2)[None], f(L0_ffn_rw2)]).reshape(E + 1, hc, P, D).transpose(2, 0, 1, 3)
    b1 = np.concatenate([f(L0_ffn_sb1)[None], f(L0_ffn_rb1)]).reshape(E + 1, hc, P).transpose(2, 0, 1)
    early = np.concatenate([f(L0_c).T, f(L0_wmod)], axis=1)
    late = np.concatenate([f(L0_attn_Wq), f(L0_attn_Wk), f(L0_attn_Wv), f(L0_ffn_router_w),
                           b1.reshape(P, -1), f(L0_ffn_sb2)[:, None]], axis=1)
    arrays = {
        "x": f(L0_attn_x), "early": early, "late": late, "router_b": f(L0_ffn_router_b)[None],
        "w1": w1, "w2": w2.reshape(P, E + 1, hc * D), "rb2": f(L0_ffn_rb2),
    }
    arrays = {k: np.ascontiguousarray(v) for k, v in arrays.items()}
    nc = bacc.Bacc("TRN2", target_bir_lowering=False, num_devices=1)
    args = [nc.dram_tensor(n, a.shape, mybir.dt.from_np(a.dtype), kind="ExternalInput").ap() for n, a in arrays.items()]
    out = nc.dram_tensor("out", arrays["x"].shape, F32, kind="ExternalOutput").ap()
    adaln_attention_moe(nc, *args, out)
    r = run_bass_kernel_spmd(nc, [arrays], core_ids=[0])
    return r.results[0]["out"]
```
